# Optimizing a Trainium2 kernel written in Bass

```python
import numpy as np
import jax
import jax.numpy as jnp

def _softmax(x, axis=-1):
    return jax.nn.softmax(x, axis=axis)

def _gelu(x):
    return jax.nn.gelu(x, approximate=True)

def _silu(x):
    return jax.nn.silu(x)

def _sigmoid(x):
    return jax.nn.sigmoid(x)

def _layernorm(x, axis=-1, eps=1e-05):
    m = jnp.mean(x, axis=axis, keepdims=True)
    v = jnp.var(x, axis=axis, keepdims=True)
    return (x - m) / jnp.sqrt(v + eps)

def _scatter_add(tgt, idx, src, axis=0):
    return tgt.at[idx].add(src)

def _segment_sum(src, seg, n):
    return jax.ops.segment_sum(src, seg, n)
kernel_name = 'mk_decoder_postln_d1_seqx_r8_9d1c9c'

def setup_inputs(seed: int=0):
    np.random.seed(seed)
    _w = jnp.asarray

    def _rec_inputs():
        import jax
        import jax.numpy as jnp
        _rk = jax.random.key(seed)
        x = -0.0002928 + 1 * jax.random.normal(jax.random.fold_in(_rk, 1), (4, 256, 512), jnp.float32)
        _lenS = 256 - jax.random.randint(jax.random.fold_in(_rk, 7), (4,), 0, max(1, 256 // 4) + 1, jnp.int32)
        _lenS2 = 1601 - jax.random.randint(jax.random.fold_in(_rk, 8), (4,), 0, max(1, 1601 // 4) + 1, jnp.int32)
        _ctx_4096P = jax.random.normal(jax.random.fold_in(_rk, 11), (4, 16, 512), jnp.float32)
        _ctx_4096c = jax.random.dirichlet(jax.random.fold_in(_rk, 511), 0.3 * jnp.ones((16,), jnp.float32), (4, 1601))
        _ctx_4096t = jnp.einsum('bsk,bkd->bsd', _ctx_4096c, _ctx_4096P)
        _ctx_4096t = _ctx_4096t * jax.lax.rsqrt(jnp.mean(jnp.square(_ctx_4096t)) + 1e-12) * 0.953939
        ctx_4096 = -2.8382e-05 + 0.999851 * (_ctx_4096t + 0.3 * jax.random.normal(jax.random.fold_in(_rk, 611), (4, 1601, 512), jnp.float32))
        _validS = jnp.arange(256)[None, :] < _lenS[:, None]
        _validS2 = jnp.arange(1601)[None, :] < _lenS2[:, None]
        _causal = jnp.tril(jnp.ones((256, 256), dtype=bool))
        mask_1x1xSxS2_ff0 = jnp.where(jnp.ones((1, 1, 256, 1601), dtype=bool), 0.0, -1000000000.0).astype(jnp.float32)
        return (x, ctx_4096, mask_1x1xSxS2_ff0)
    x, ctx_4096, mask_1x1xSxS2_ff0 = _rec_inputs()

    def _L0_attn_setup():
        import jax, jax.numpy as jnp
        import numpy as np
        K_FACTOR = 0.5
        key = jax.random.key(seed)
        k1, k2, k3, k4 = jax.random.split(key, 4)
        B, S, H, I = (1, 256, 512, 1376)
        x = jax.random.normal(k1, (B, S, H), dtype=jnp.float32)
        w_gate = jax.random.normal(k2, (I, H), dtype=jnp.float32) * 0.02
        w_up = jax.random.normal(k3, (I, H), dtype=jnp.float32) * 0.02
        w_down = jax.random.normal(k4, (H, I), dtype=jnp.float32) * 0.02
        return {'x': x, 'w_gate': w_gate, 'w_up': w_up, 'w_down': w_down}
    _L0_attn_all = _L0_attn_setup()
    _L0_attn_in = {k: v for k, v in _L0_attn_all.items() if k in ('w_gate', 'w_up', 'w_down')}
    del _L0_attn_all

    def _L0_xattn_setup():
        import jax, jax.numpy as jnp
        import numpy as np
        B, Q, K, D = (1, 128, 6404, 512)
        H, KVH, HD = (32, 8, 128)
        GROUPS = H // KVH
        EPS = 1e-05

        def _rmsnorm(x, w):
            xf = x.astype(jnp.float32)
            var = jnp.mean(xf * xf, axis=-1, keepdims=True)
            return (xf * jax.lax.rsqrt(var + EPS)).astype(x.dtype) * w
        key = jax.random.key(seed)
        ks = jax.random.split(key, 8)
        s = 0.02
        return {'hidden_states': jax.random.normal(ks[0], (B, Q, D), jnp.float32), 'cross_attention_states': jax.random.normal(ks[1], (B, K, D), jnp.float32), 'attention_mask': jnp.zeros((B, 1, Q, K), jnp.float32), 'Wq': jax.random.normal(ks[2], (H * HD, D), jnp.float32) * s, 'Wk': jax.random.normal(ks[3], (KVH * HD, D), jnp.float32) * s, 'Wv': jax.random.normal(ks[4], (KVH * HD, D), jnp.float32) * s, 'Wo': jax.random.normal(ks[5], (D, H * HD), jnp.float32) * s, 'q_norm_w': jnp.ones((HD,), jnp.float32), 'k_norm_w': jnp.ones((HD,), jnp.float32)}
    _L0_xattn_all = _L0_xattn_setup()
    _L0_xattn_in = {k: v for k, v in _L0_xattn_all.items() if k in ('Wq', 'Wk', 'Wv', 'Wo', 'q_norm_w', 'k_norm_w')}
    del _L0_xattn_all

    def _L0_ffn_setup():
        import jax, jax.numpy as jnp
        import numpy as np
        R = 16
        LORA_ALPHA = 16
        SCALING = LORA_ALPHA / R
        key = jax.random.key(seed)
        kx, kr, ka = jax.random.split(key, 3)
        B, S, D, DO, E = (4, 256, 512, 512, 8)
        x = jax.random.normal(kx, (B, S, D), dtype=jnp.float32)
        bound_r = 1.0 / np.sqrt(D)
        route_w = jax.random.uniform(kr, (E, D), jnp.float32, -bound_r, bound_r)
        bound_a = 1.0 / np.sqrt(D)
        A = jax.random.uniform(ka, (E, R, D), jnp.float32, -bound_a, bound_a)
        kb = jax.random.fold_in(key, 7)
        Bw = jax.random.normal(kb, (E, DO, R), dtype=jnp.float32) * 0.02
        return {'x': x, 'route_w': route_w, 'A': A, 'Bw': Bw}
    _L0_ffn_all = _L0_ffn_setup()
    _L0_ffn_in = {k: v for k, v in _L0_ffn_all.items() if k in ('route_w', 'A', 'Bw')}
    del _L0_ffn_all
    return {'x': x, 'ctx_4096': ctx_4096, 'mask_1x1xSxS2_ff0': mask_1x1xSxS2_ff0, 'L0_attn_w_gate': _L0_attn_in['w_gate'], 'L0_attn_w_up': _L0_attn_in['w_up'], 'L0_attn_w_down': _L0_attn_in['w_down'], 'L0_xattn_Wq': _L0_xattn_in['Wq'], 'L0_xattn_Wk': _L0_xattn_in['Wk'], 'L0_xattn_Wv': _L0_xattn_in['Wv'], 'L0_xattn_Wo': _L0_xattn_in['Wo'], 'L0_xattn_q_norm_w': _L0_xattn_in['q_norm_w'], 'L0_xattn_k_norm_w': _L0_xattn_in['k_norm_w'], 'L0_ffn_route_w': _L0_ffn_in['route_w'], 'L0_ffn_A': _L0_ffn_in['A'], 'L0_ffn_Bw': _L0_ffn_in['Bw']}

def reference(x, ctx_4096, mask_1x1xSxS2_ff0, L0_attn_w_gate, L0_attn_w_up, L0_attn_w_down, L0_xattn_Wq, L0_xattn_Wk, L0_xattn_Wv, L0_xattn_Wo, L0_xattn_q_norm_w, L0_xattn_k_norm_w, L0_ffn_route_w, L0_ffn_A, L0_ffn_Bw):
    import jax
    import jax.numpy as jnp

    def _L0_attn_ref(x, w_gate, w_up, w_down):
        import jax, jax.numpy as jnp
        import numpy as np
        K_FACTOR = 0.5
        s = jax.nn.silu(jnp.einsum('bsh,ih->bsi', x, w_gate))
        B, S, I = s.shape
        k = int(K_FACTOR * I)
        _, idx = jax.lax.top_k(-jnp.abs(s), k)
        flat = s.reshape(B * S, I)
        rows = jnp.arange(B * S)[:, None]
        flat = flat.at[rows, idx.reshape(B * S, k)].set(0.0)
        s = flat.reshape(B, S, I)
        s = s * jnp.einsum('bsh,ih->bsi', x, w_up)
        return jnp.einsum('bsi,hi->bsh', s, w_down)

    def _L0_xattn_ref(hidden_states, cross_attention_states, attention_mask, Wq, Wk, Wv, Wo, q_norm_w, k_norm_w):
        import jax, jax.numpy as jnp
        import numpy as np
        B, Q, K, D = (1, 128, 6404, 512)
        H, KVH, HD = (32, 8, 128)
        GROUPS = H // KVH
        EPS = 1e-05

        def _rmsnorm(x, w):
            xf = x.astype(jnp.float32)
            var = jnp.mean(xf * xf, axis=-1, keepdims=True)
            return (xf * jax.lax.rsqrt(var + EPS)).astype(x.dtype) * w
        bsz, q_len, _ = hidden_states.shape
        kv_len = cross_attention_states.shape[1]
        q = (hidden_states @ Wq.T).reshape(bsz, q_len, H, HD).transpose(0, 2, 1, 3)
        k = (cross_attention_states @ Wk.T).reshape(bsz, kv_len, KVH, HD).transpose(0, 2, 1, 3)
        v = (cross_attention_states @ Wv.T).reshape(bsz, kv_len, KVH, HD).transpose(0, 2, 1, 3)
        q = _rmsnorm(q, q_norm_w)
        k = jnp.repeat(k, GROUPS, axis=1)
        v = jnp.repeat(v, GROUPS, axis=1)
        k = _rmsnorm(k, k_norm_w)
        scale = 1.0 / np.sqrt(HD)
        scores = jnp.einsum('bhqd,bhkd->bhqk', q, k) * scale
        scores = scores + attention_mask[:, :, :, :kv_len]
        probs = jax.nn.softmax(scores.astype(jnp.float32), axis=-1).astype(q.dtype)
        out = jnp.einsum('bhqk,bhkd->bhqd', probs, v)
        out = out.transpose(0, 2, 1, 3).reshape(bsz, q_len, H * HD)
        return out @ Wo.T

    def _L0_ffn_ref(x, route_w, A, Bw):
        import jax, jax.numpy as jnp
        import numpy as np
        R = 16
        LORA_ALPHA = 16
        SCALING = LORA_ALPHA / R
        logits = jnp.einsum('bsd,ed->bse', x, route_w)
        topk_v, topk_idx = jax.lax.top_k(logits, 1)
        E = logits.shape[-1]
        route_weight = jax.nn.one_hot(topk_idx[..., 0], E, dtype=logits.dtype) * topk_v
        h = jnp.einsum('bsd,erd->bser', x, A)
        wh = route_weight[..., None] * h
        out = jnp.einsum('bser,eor->bso', wh, Bw) * SCALING
        return out
    x = _layernorm(x + _L0_attn_ref(x, L0_attn_w_gate, L0_attn_w_up, L0_attn_w_down), axis=-1)
    x = _layernorm(x + _L0_xattn_ref(x, ctx_4096, mask_1x1xSxS2_ff0, L0_xattn_Wq, L0_xattn_Wk, L0_xattn_Wv, L0_xattn_Wo, L0_xattn_q_norm_w, L0_xattn_k_norm_w), axis=-1)
    x = _layernorm(x + _L0_ffn_ref(x, L0_ffn_route_w, L0_ffn_A, L0_ffn_Bw), axis=-1)
    return x

_drawn_inputs = setup_inputs


def setup_inputs(seed=0):
    import zlib

    import numpy as np

    out = dict(_drawn_inputs(seed))
    spreads = {'L0_xattn_q_norm_w': (1.0, 0.6), 'L0_xattn_k_norm_w': (1.0, 0.6)}
    factors = {}
    for name, (base, spread) in spreads.items():
        noise = np.random.default_rng([zlib.crc32(name.encode()), seed]).standard_normal(out[name].shape)
        drawn = base * np.exp(spread * noise) if base else spread * noise
        out[name] = jnp.asarray(drawn.astype(out[name].dtype))
    for name, factor in factors.items():
        out[name] = (out[name] * factor).astype(out[name].dtype)
    return out
```

```python
from contextlib import ExitStack

import concourse.bass as bass
from concourse import mybir
from concourse.alu_op_type import AluOpType as ALU

ACT = mybir.ActivationFunctionType
F32 = mybir.dt.float32
BF16 = mybir.dt.bfloat16
F32R = mybir.dt.float32r
U32 = mybir.dt.uint32

P = 128
B, S, D = 4, 256, 512
KV = 1601
I = 1376
H, G, HD = 32, 8, 128
E, R = 8, 16
T = B * S
TT = T // P
CT = D // P
NK = B * KV
DROP = I // 2
EPS = 1e-5

GB, GW = 3, 460
IP = GB * GW
IC = (I + P - 1) // P
IR = I - (IC - 1) * P
KT = (NK + P - 1) // P
LAST_KEY = NK - P


def cols(ap, width=P):
    return ap.rearrange("(c p) n -> p c n", p=width)


AHEAD = 32


def done(step):
    return AHEAD + 1 + step


def landed(step):
    return 16 * (AHEAD + 1 + step)


def begin(eng, *sems):
    for x in sems:
        eng.sem_inc(x, AHEAD)


def begin_dma(eng, *sems):
    for x in sems:
        eng.sem_inc(x, 16 * AHEAD)


def wait_apart(eng, sem, value, passed):
    eng.wait_ge(sem, value)
    eng.sem_inc(passed, 1)


class Chain:

    def __init__(self, eng, sem, base=0):
        self.eng, self.sem, self.base, self.n = eng, sem, base, 0

    def done(self, ins):
        self.n += 1
        ins.then_inc(self.sem, 1)

    def wait(self, behind=0):
        self.eng.wait_ge(self.sem, self.base + self.n - behind)

    def wait_apart(self, passed):
        wait_apart(self.eng, self.sem, self.base + self.n, passed)


def product(pe, out, a_hi, a_lo, b_hi, b_lo, start, stop):
    pe.matmul(out, a_hi, b_hi, start=start, stop=False)
    pe.matmul(out, a_hi, b_lo, start=False, stop=False)
    return pe.matmul(out, a_lo, b_hi, start=False, stop=stop)


def gate_and_up(nc, psum, abs_s, xT, WgT, WuT, pS):
    with ExitStack() as ctx:
        def sb(name, shape, dt=F32):
            return ctx.enter_context(nc.sbuf_tensor(name, shape, dt))

        def sem(name):
            return ctx.enter_context(nc.semaphore(name))

        RAW = 4
        w_raw = sb("w_raw", [P, RAW, I])
        w_hi = sb("w_hi", [P, 2, CT, IP], F32R)
        w_lo = sb("w_lo", [P, 2, CT, IP], F32R)
        x_raw = sb("x_raw", [P, 2, CT, P])
        x_hi = sb("x_hi", [P, 2, CT, P], F32R)
        x_lo = sb("x_lo", [P, 2, CT, P], F32R)
        s_sb = sb("s_sb", [P, 2, IP])
        p_sb = sb("p_sb", [P, 2, IP])

        w_in = [sem(f"w_in{n}") for n in range(RAW)]
        w_hi_done, w_lo_done, pads = sem("w_hi_done"), sem("w_lo_done"), sem("pads")
        x_in = [sem(f"x_in{s}") for s in range(2)]
        x_hi_done, x_lo_done = sem("x_hi_done"), sem("x_lo_done")
        g_done, u_done = sem("g_done"), sem("u_done")
        s_done, p_done, abs_done = sem("s_done"), sem("p_done"), sem("abs_done")
        p_out = [sem(f"p_out{s}") for s in range(2)]

        g_ps, u_ps = psum[:, 0:GB, 0:GW], psum[:, GB:2 * GB, 0:GW]
        weights = [cols(WgT), cols(WuT)]
        block = ctx.enter_context(nc.Block())

        @block.sync
        def _(sp):
            begin_dma(sp, *x_in, *p_out)

            def load_x(t, s):
                sp.dma_start(x_raw[:, s], cols(xT)[:, :, bass.ds(t * P, P)]).then_inc(x_in[s], 16)

            def store_p(t, s):
                sp.wait_ge(p_done, done(t))
                sp.dma_start(pS[t], p_sb[:, s, 0:I]).then_inc(p_out[s], 16)

            for n in range(2 * CT):
                if n == 1:
                    load_x(0, 0)
                    load_x(1, 1)
                if n >= RAW:
                    sp.wait_ge(w_lo_done, n - RAW + 1)
                sp.dma_start(w_raw[:, n % RAW, :], weights[n // CT][:, n % CT, :]).then_inc(w_in[n % RAW], 16)
            with sp.Fori(0, TT // 2 - 1) as i:
                for s in range(2):
                    sp.wait_ge(x_lo_done, done(2 * i + s))
                    load_x(2 * i + s + 2, s)
                    store_p(2 * i + s, s)
            for t in (TT - 2, TT - 1):
                store_p(t, t % 2)
            for s in range(2):
                sp.wait_ge(p_out[s], landed(TT // 2 - 1))

        @block.gpsimd
        def _(pool):
            begin(pool, x_lo_done)
            pool.memset(w_hi[:, :, :, I:IP].bitcast(F32), 0.0).then_inc(pads, 1)
            pool.memset(w_lo[:, :, :, I:IP].bitcast(F32), 0.0).then_inc(pads, 1)
            with pool.Fori(0, TT // 2) as i:
                for s in range(2):
                    pool.wait_ge(x_hi_done, done(2 * i + s))
                    pool.tensor_tensor(x_lo[:, s], x_raw[:, s], x_hi[:, s].bitcast(F32), ALU.subtract
                                       ).then_inc(x_lo_done, 1)

        @block.scalar
        def _(act):
            begin(act, x_hi_done, s_done)

            def split_x(t, s, i):
                act.wait_ge(x_in[s], landed(i))
                act.wait_ge(u_done, done(t - 2))
                act.copy(x_hi[:, s], x_raw[:, s]).then_inc(x_hi_done, 1)

            def silu(t, s):
                act.wait_ge(g_done, done(t))
                act.wait_ge(p_done, done(t - 2))
                act.activation(s_sb[:, s].rearrange("p (b n) -> p b n", b=GB), g_ps, ACT.Silu
                               ).then_inc(s_done, 1)

            for n in range(2 * CT):
                act.wait_ge(w_in[n % RAW], 16 * (n // RAW + 1))
                act.copy(w_hi[:, n // CT, n % CT, 0:I], w_raw[:, n % RAW, :]).then_inc(w_hi_done, 1)
                if n == 0:
                    split_x(0, 0, 0)
            silu(0, 0)
            split_x(1, 1, 0)
            silu(1, 1)
            with act.Fori(1, TT // 2) as i:
                for s in range(2):
                    split_x(2 * i + s, s, i)
                    silu(2 * i + s, s)

        @block.vector
        def _(dve):
            begin(dve, p_done, abs_done)
            for n in range(2 * CT):
                dve.wait_ge(w_hi_done, n + 1)
                dve.tensor_tensor(w_lo[:, n // CT, n % CT, 0:I], w_raw[:, n % RAW, :],
                                  w_hi[:, n // CT, n % CT, 0:I].bitcast(F32), ALU.subtract
                                  ).then_inc(w_lo_done, 1)
            with dve.Fori(0, TT // 2) as i:
                for s in range(2):
                    t = 2 * i + s
                    dve.wait_ge(s_done, done(t))
                    dve.tensor_scalar(abs_s[:, t, :].bitcast(U32), s_sb[:, s, 0:I].bitcast(U32),
                                      0x7FFFFFFF, None, ALU.bitwise_and).then_inc(abs_done, 1)
                    dve.wait_ge(u_done, done(t))
                    dve.wait_ge(p_out[s], landed(i - 1))
                    dve.tensor_tensor(p_sb[:, s].rearrange("p (b n) -> p b n", b=GB), u_ps,
                                      s_sb[:, s].rearrange("p (b n) -> p b n", b=GB), ALU.mult
                                      ).then_inc(p_done, 1)

        @block.tensor
        def _(pe):
            begin(pe, g_done, u_done)
            pe.wait_ge(pads, 2)
            with pe.Fori(0, TT // 2) as i:
                for s in range(2):
                    t = 2 * i + s
                    pe.wait_ge(x_lo_done, done(t))
                    for m, free, ready in ((0, s_done, g_done), (1, p_done, u_done)):
                        pe.wait_ge(free, done(t - 1))
                        for c in range(CT):
                            pe.wait_ge(w_lo_done, CT * m + c + 1)
                            for b in range(GB):
                                w = slice(b * GW, (b + 1) * GW)
                                last = product(pe, psum[:, GB * m + b, 0:GW], x_hi[:, s, c], x_lo[:, s, c],
                                               w_hi[:, m, c, w], w_lo[:, m, c, w], c == 0, c == CT - 1)
                        last.then_inc(ready, 1)


def keys_and_values(nc, psum, ident, abs_s, thr, n_less, ctxT, WkT, WvT, kS, vS):
    with ExitStack() as ctx:
        def sb(name, shape, dt=F32):
            return ctx.enter_context(nc.sbuf_tensor(name, shape, dt))

        def sem(name):
            return ctx.enter_context(nc.semaphore(name))

        N = G * HD
        NB = N // 512
        RING = 3
        STEPS = KT // RING - 1
        BITS = 2
        assert KT == RING * (STEPS + 1) and BITS * STEPS >= 31
        w_raw = sb("kvw_raw", [P, 2, 512])
        w_hi = sb("kvw_hi", [P, 2 * NB, CT, 512], F32R)
        w_lo = sb("kvw_lo", [P, 2 * NB, CT, 512], F32R)
        c_raw = sb("c_raw", [P, RING, CT, P])
        c_hi = sb("c_hi", [P, RING, CT, P], F32R)
        c_lo = sb("c_lo", [P, RING, CT, P], F32R)
        square = sb("square", [P, N])
        ssq = sb("ssq", [P, RING, G])
        var = sb("var", [P, RING, G])
        rstd = sb("rstd", [P, RING, G])
        minus_half = sb("minus_half", [P, G])
        k_sb = sb("k_sb", [P, N])
        v_sb = sb("v_sb", [P, 2, N])
        kT_sb = sb("kT_sb", [P, 2, N])
        bit = sb("bit", [P, TT], U32)
        cand = sb("cand", [P, TT], U32)
        less = sb("less", [P, TT])
        below = sb("below", [P, TT], U32)
        flags = sb("flags", [P, 2, I], BF16)

        w_in = [sem(f"kvw_in{s}") for s in range(2)]
        w_hi_done, w_lo_done, half = sem("kvw_hi_done"), sem("kvw_lo_done"), sem("half")
        c_in = [sem(f"c_in{s}") for s in range(RING)]
        c_hi_done, c_lo_done = sem("c_hi_done"), sem("c_lo_done")
        k_done, v_done, kT_done = sem("k_done"), sem("v_done"), sem("kT_done")
        ssq_done, var_done, rstd_done = sem("ssq_done"), sem("var_done"), sem("rstd_done")
        k_sb_done, v_sb_done, kT_sb_done = sem("k_sb_done"), sem("v_sb_done"), sem("kT_sb_done")
        v_out = [sem(f"v_out{s}") for s in range(2)]
        kT_out = [sem(f"kT_out{s}") for s in range(2)]
        chain = sem("bit_chain")
        pool_passed, dve_passed, sp_passed = sem("pool_passed_k"), sem("dve_passed_k"), sem("sp_passed_k")

        def k_banks(s):
            return psum[:, NB * s:NB * s + NB, :].rearrange("p b n -> p (b n)")

        v_bank = NB * RING
        v_ps = psum[:, v_bank:v_bank + NB, :].rearrange("p b n -> p (b n)")
        block = ctx.enter_context(nc.Block())

        BODY = 2 * RING
        TRIPS = STEPS // 2

        def tiles(eng, step, trips=TRIPS):
            with eng.Fori(0, trips) as i:
                for s in range(BODY):
                    step(i, s)
            for t in range(BODY * trips, KT):
                step(t // BODY, t % BODY)

        def fresh(i, s):
            t = BODY * i + s
            return (LAST_KEY, KT * P - NK) if isinstance(i, int) and t == KT - 1 else (t * P, 0)

        def is_tile(i, s):
            return not isinstance(i, int) or BODY * i + s < KT

        @block.sync
        def _(sp):
            begin_dma(sp, *c_in, *v_out, *kT_out)

            def load_c(i, s):
                sp.wait_ge(c_lo_done, done(BODY * i + s - RING))
                sp.dma_start(c_raw[:, s % RING], cols(ctxT)[:, :, bass.ds(fresh(i, s)[0], P)]
                             ).then_inc(c_in[s % RING], 16)

            def store(i, s):
                t, r = BODY * i + s, s % 2
                start, old = fresh(i, s)
                at = bass.ds(start + old, P - old)
                sp.wait_ge(v_sb_done, done(t))
                sp.dma_start(vS[at, :], v_sb[old:P, r]).then_inc(v_out[r], 16)
                wait_apart(sp, kT_sb_done, done(t), sp_passed)
                sp.dma_start(kS[:, :, at].rearrange("g d k -> d g k"),
                             kT_sb[:, r].rearrange("d (g k) -> d g k", g=G)[:, :, old:P]).then_inc(kT_out[r], 16)

            for n in range(2 * NB * CT):
                if n == 2:
                    for t in range(RING):
                        load_c(0, t)
                if n >= 2:
                    sp.wait_ge(w_lo_done, n - 1)
                j, c = n // CT % NB, n % CT
                src = (WkT, WvT)[n // (NB * CT)]
                sp.dma_start(w_raw[:, n % 2], cols(src)[:, c, j * 512:(j + 1) * 512]).then_inc(w_in[n % 2], 16)

            def step(i, s):
                if is_tile(i, s + RING):
                    load_c(i, s + RING)
                store(i, s)

            tiles(sp, step, TRIPS - 1)
            for s in range(2):
                sp.wait_ge(v_out[s], landed((KT - 1 - s) // 2))
                sp.wait_ge(kT_out[s], landed((KT - 1 - s) // 2))

        @block.gpsimd
        def _(pool):
            begin(pool, c_lo_done, var_done, rstd_done)
            pool.memset(minus_half[:], -0.5).then_inc(half, 1)
            pool.wait_ge(half, 1)

            def split_c(i, s):
                pool.wait_ge(c_hi_done, done(BODY * i + s))
                pool.tensor_tensor(c_lo[:, s % RING], c_raw[:, s % RING], c_hi[:, s % RING].bitcast(F32),
                                   ALU.subtract).then_inc(c_lo_done, 1)

            def step(i, s):
                t, r = BODY * i + s, s % RING
                wait_apart(pool, ssq_done, done(t), pool_passed)
                pool.tensor_scalar(var[:, r], ssq[:, r], 1.0 / HD, EPS, ALU.mult, ALU.add).then_inc(var_done, 1)
                pool.wait_ge(var_done, done(t))
                pool.tensor_tensor(rstd[:, r], var[:, r], minus_half[:], ALU.pow).then_inc(rstd_done, 1)
                if is_tile(i, s + 2):
                    split_c(i, s + 2)

            split_c(0, 0)
            split_c(0, 1)
            tiles(pool, step)

        @block.scalar
        def _(act):
            begin(act, c_hi_done, ssq_done, v_sb_done, kT_sb_done)

            def split_c(i, s):
                act.wait_ge(c_in[s % RING], landed(2 * i + s // RING))
                act.wait_ge(v_done, done(BODY * i + s - RING))
                act.copy(c_hi[:, s % RING], c_raw[:, s % RING]).then_inc(c_hi_done, 1)

            split_c(0, 0)
            split_c(0, 1)
            for n in range(2 * NB * CT):
                act.wait_ge(w_in[n % 2], 16 * (n // 2 + 1))
                act.copy(w_hi[:, n // CT, n % CT], w_raw[:, n % 2]).then_inc(w_hi_done, 1)

            def step(i, s):
                t, use2 = BODY * i + s, BODY // 2 * i + s // 2
                act.wait_ge(k_done, done(t))
                act.wait_ge(ssq_done, done(t - 1))
                for g in range(G):
                    last = act.activation(square[:, g * HD:(g + 1) * HD], k_banks(s % RING)[:, g * HD:(g + 1) * HD], ACT.Square,
                                          accum_out=ssq[:, s % RING, g:g + 1])
                last.then_inc(ssq_done, 1)
                act.wait_ge(v_done, done(t))
                act.wait_ge(v_out[s % 2], landed(use2 - 1))
                act.copy(v_sb[:, s % 2], v_ps).then_inc(v_sb_done, 1)
                if is_tile(i, s + 2):
                    split_c(i, s + 2)
                act.wait_ge(kT_done, done(t))
                act.wait_ge(kT_out[s % 2], landed(use2 - 1))
                act.copy(kT_sb[:, s % 2], k_banks(s % RING)).then_inc(kT_sb_done, 1)

            tiles(act, step)

        @block.vector
        def _(dve):
            begin(dve, k_sb_done)
            for n in range(2 * NB * CT):
                dve.wait_ge(w_hi_done, n + 1)
                dve.tensor_tensor(w_lo[:, n // CT, n % CT], w_raw[:, n % 2], w_hi[:, n // CT, n % CT].bitcast(F32),
                                  ALU.subtract).then_inc(w_lo_done, 1)
            bits = Chain(dve, chain)
            bits.done(dve.memset(thr[:].bitcast(F32), 0.0))
            bits.done(dve.memset(bit[:].bitcast(F32), 2.0))

            def count(at, tt, out):
                bits.wait(behind=1)
                bits.done(dve.tensor_scalar(flags[:, tt % 2], abs_s[:, tt], at[:, tt:tt + 1].bitcast(F32), 0.0,
                                            ALU.is_lt, ALU.add, accum_out=out[:, tt:tt + 1]))

            def norm_keys(i, s):
                t = BODY * i + s
                dve.wait_ge(rstd_done, done(t))
                dve.wait_ge(kT_done, done(t - 1))
                dve.tensor_tensor(k_sb[:].rearrange("p (g d) -> p g d", g=G),
                                  k_banks(s % RING).rearrange("p (g d) -> p g d", g=G),
                                  rstd[:, s % RING].unsqueeze(2).to_broadcast((P, G, HD)), ALU.mult
                                  ).then_inc(k_sb_done, 1)

            first = bits.n
            with dve.Fori(0, TRIPS) as i:
                per_trip = BITS * 2 * (TT + 4)
                bits.base, bits.n = first + per_trip * i, 0
                for s in range(BODY):
                    norm_keys(i, s)
                    for q in range(BITS * 2 * TT * s // BODY, BITS * 2 * TT * (s + 1) // BODY):
                        if q % TT == 0:
                            bits.wait()
                            bits.done(dve.tensor_tensor(cand[:], thr[:], bit[:], ALU.bitwise_or))
                            bits.wait()
                        count(cand, q % TT, less)
                        if q % TT == TT - 1:
                            bits.done(dve.tensor_scalar(bit[:], bit[:], 1, None, ALU.logical_shift_right))
                            bits.wait()
                            bits.done(dve.tensor_scalar(below[:], less[:], DROP - 0.5, None, ALU.is_lt))
                            bits.wait_apart(dve_passed)
                            bits.done(dve.copy_predicated(thr[:], below[:], cand[:]))
                assert bits.n == per_trip
            bits.base, bits.n = first, per_trip * TRIPS
            bits.wait()
            for s in range(KT - BODY * TRIPS):
                norm_keys(TRIPS, s)
                for tt in range(TT * s // 3, TT * (s + 1) // 3):
                    count(thr, tt, n_less)
            bits.wait()

        @block.tensor
        def _(pe):
            begin(pe, k_done, v_done, kT_done)

            def project(i, s, which, out, first=False):
                for j in range(NB):
                    for c in range(CT):
                        m = NB * which + j
                        if first:
                            pe.wait_ge(w_lo_done, CT * m + c + 1)
                        last = product(pe, out[:, j * 512:(j + 1) * 512], c_hi[:, s % RING, c], c_lo[:, s % RING, c],
                                       w_hi[:, m, c], w_lo[:, m, c], c == 0, c == CT - 1)
                return last

            def keys(i, s, first=False):
                pe.wait_ge(c_lo_done, done(BODY * i + s))
                pe.wait_ge(kT_sb_done, done(BODY * i + s - RING))
                project(i, s, 0, k_banks(s % RING), first).then_inc(k_done, 1)

            def values(i, s, first=False):
                pe.wait_ge(v_sb_done, done(BODY * i + s - 1))
                project(i, s, 1, v_ps, first).then_inc(v_done, 1)

            def transpose(i, s):
                pe.wait_ge(k_sb_done, done(BODY * i + s))
                for g in range(G):
                    last = pe.transpose(k_banks(s % RING)[:, g * P:(g + 1) * P], k_sb[:, g * HD:(g + 1) * HD], ident)
                last.then_inc(kT_done, 1)

            def step(i, s):
                if is_tile(i, s + 1):
                    keys(i, s + 1)
                transpose(i, s)
                if is_tile(i, s + 1):
                    values(i, s + 1)

            keys(0, 0, True)
            values(0, 0, True)
            tiles(pe, step)


def make_identity(nc, ident):
    with nc.semaphore("ident_done") as ident_done, nc.Block() as block:
        @block.gpsimd
        def _(pool):
            pool.memset(ident, 0.0).then_inc(ident_done, 1)
            pool.wait_ge(ident_done, 1)
            pool.affine_select(out=ident, in_=ident, compare_op=ALU.not_equal, fill=1.0, base=0,
                               pattern=[[-1, P]], channel_multiplier=1).then_inc(ident_done, 1)
            pool.wait_ge(ident_done, 2)


def down_and_norm(nc, psum, ident, abs_s, thr, n_less, x1T_hi, x1T_lo, x, WdT, pS, x1S):
    with ExitStack() as ctx:
        def sb(name, shape, dt=F32):
            return ctx.enter_context(nc.sbuf_tensor(name, shape, dt))

        def sem(name):
            return ctx.enter_context(nc.semaphore(name))

        w_raw = sb("wd_raw", [P, 2, D])
        w_hi = sb("wd_hi", [P, IC, D], F32R)
        w_lo = sb("wd_lo", [P, IC, D], F32R)
        p_sb = sb("pd_sb", [P, 2, I])
        x_sb = sb("xd_sb", [P, 2, D])
        need = sb("need", [P, TT])
        equal = sb("equal", [P, I])
        order = sb("order", [P, I])
        keep = sb("keep", [P, I])
        h_sb = sb("h_sb", [P, 2, IC * P])
        hT_hi = sb("hT_hi", [P, 2, IC * P], F32R)
        hT_lo = sb("hT_lo", [P, 2, IC * P], F32R)
        y_sb = sb("yd_sb", [P, 2, D])
        stats = sb("stats_d", [P, 2, 6])
        mv = sb("mv_d", [P, 2, 2])
        rstd = sb("rstd_d", [P, 2])
        minus_half = sb("minus_half_d", [P, 1])
        x1_sb = sb("x1_sb", [P, 2, D])

        w_in = [sem(f"wd_in{s}") for s in range(2)]
        p_in = [sem(f"pd_in{s}") for s in range(2)]
        x_in = [sem(f"xd_in{s}") for s in range(2)]
        w_hi_done, w_lo_done, pads, w_pads = sem("wd_hi_done"), sem("wd_lo_done"), sem("pads_d"), sem("w_pads")
        chain = sem("chain_d")
        keep_done, h_done, hT_done = sem("keep_done"), sem("h_done"), sem("hT_done")
        hT_hi_done, hT_lo_done = sem("hT_hi_done"), sem("hT_lo_done")
        down_done, mv_done, rstd_done = sem("down_done"), sem("mv_done"), sem("rstd_done_d")
        x1_done, x1T_done, x1T_hi_done, x1T_lo_done = (sem("x1_done"), sem("x1T_done"), sem("x1T_hi_done"),
                                                       sem("x1T_lo_done"))
        x1_out = [sem(f"x1_out{s}") for s in range(2)]
        dve_passed = sem("dve_passed_d")

        def hT_ps(s):
            return psum[:, 3 * s:3 * s + 3, :].rearrange("p b n -> p (b n)")[:, 0:IC * P]

        def y_ps(s):
            return psum[:, 6 + s, :]

        def tiles(eng, step):
            with eng.Fori(0, TT // 2) as i:
                for s in range(2):
                    step(i, s)

        block = ctx.enter_context(nc.Block())

        @block.sync
        def _(sp):
            begin_dma(sp, *p_in, *x_in, *x1_out)
            for n in range(IC):
                rows = P if n < IC - 1 else IR
                if n == 2:
                    for s in range(2):
                        sp.dma_start(p_sb[:, s], pS[s]).then_inc(p_in[s], 16)
                        sp.dma_start(x_sb[:, s], x[s * P:(s + 1) * P, :]).then_inc(x_in[s], 16)
                if n >= 2:
                    sp.wait_ge(w_lo_done, n - 1)
                sp.dma_start(w_raw[0:rows, n % 2], WdT[n * P:n * P + rows, :]).then_inc(w_in[n % 2], 16)

            def store(i, s):
                sp.wait_ge(x1_done, done(2 * i + s))
                sp.dma_start(x1S[bass.ds((2 * i + s) * P, P), :], x1_sb[:, s]).then_inc(x1_out[s], 16)

            with sp.Fori(0, TT // 2 - 1) as i:
                for s in range(2):
                    t = 2 * i + s
                    sp.wait_ge(h_done, done(t))
                    sp.dma_start(p_sb[:, s], pS[t + 2]).then_inc(p_in[s], 16)
                    store(i, s)
                    sp.dma_start(x_sb[:, s], x[bass.ds((t + 2) * P, P), :]).then_inc(x_in[s], 16)
            for s in range(2):
                store(TT // 2 - 1, s)
            for s in range(2):
                sp.wait_ge(x1_out[s], landed(TT // 2 - 1))

        @block.gpsimd
        def _(pool):
            begin(pool, h_done, rstd_done)
            pool.memset(h_sb[:, :, I:IC * P], 0.0).then_inc(pads, 1)
            pool.memset(minus_half[:], -0.5).then_inc(pads, 1)
            pool.wait_ge(pads, 2)

            def gates(i, s):
                t = 2 * i + s
                pool.wait_ge(keep_done, done(t))
                pool.wait_ge(p_in[s], landed(i))
                pool.wait_ge(hT_done, done(t - 2))
                pool.tensor_tensor(h_sb[:, s, 0:I], p_sb[:, s], keep[:], ALU.mult).then_inc(h_done, 1)

            def root(i, s):
                pool.wait_ge(mv_done, done(2 * i + s))
                pool.tensor_tensor(rstd[:, s:s + 1], mv[:, s, 1:2], minus_half[:], ALU.pow).then_inc(rstd_done, 1)

            gates(0, 0)
            gates(0, 1)
            with pool.Fori(0, TT // 2 - 1) as i:
                for s in range(2):
                    root(i, s)
                    gates(i + 1, s)
            for s in range(2):
                root(TT // 2 - 1, s)

        @block.scalar
        def _(act):
            begin(act, hT_hi_done, x1T_hi_done)
            for n in range(IC):
                rows = P if n < IC - 1 else IR
                act.wait_ge(w_in[n % 2], 16 * (n // 2 + 1))
                act.copy(w_hi[0:rows, n], w_raw[0:rows, n % 2]).then_inc(w_hi_done, 1)

            def gates(i, s):
                t = 2 * i + s
                act.wait_ge(hT_done, done(t))
                act.wait_ge(down_done, done(t - 2))
                act.copy(hT_hi[:, s], hT_ps(s)).then_inc(hT_hi_done, 1)

            def x1(i, s):
                t = 2 * i + s
                act.wait_ge(x1T_done, done(t))
                act.copy(x1T_hi[:, :, bass.ds(t * P, P)], y_ps(s).rearrange("p (c n) -> p c n", c=CT)
                         ).then_inc(x1T_hi_done, 1)

            gates(0, 0)
            gates(0, 1)
            with act.Fori(0, TT // 2 - 1) as i:
                for s in range(2):
                    x1(i, s)
                    gates(i + 1, s)
            for s in range(2):
                x1(TT // 2 - 1, s)

        @block.vector
        def _(dve):
            begin(dve, keep_done, hT_lo_done, mv_done, x1_done, x1T_lo_done)
            dve.memset(w_hi[IR:P, IC - 1, :].bitcast(F32), 0.0).then_inc(w_pads, 1)
            dve.memset(w_lo[IR:P, IC - 1, :].bitcast(F32), 0.0).then_inc(w_pads, 1)
            own = Chain(dve, chain)
            own.done(dve.tensor_scalar(need[:], n_less[:], -1.0, float(DROP), ALU.mult, ALU.add))

            def choose(i, s):
                t = 2 * i + s
                at = thr[:, bass.ds(t, 1)].bitcast(F32)
                own.wait()
                own.done(dve.tensor_scalar(equal[:], abs_s[:, t], at, None, ALU.is_equal))
                own.wait()
                own.done(dve.tensor_tensor_scan(order[:], equal[:], equal[:], 0.0, ALU.add, ALU.max))
                own.wait()
                own.done(dve.scalar_tensor_tensor(order[:], order[:], need[:, bass.ds(t, 1)], equal[:],
                                                  ALU.is_gt, ALU.mult))
                own.wait()
                dve.wait_ge(h_done, done(t - 1))
                dve.scalar_tensor_tensor(keep[:], abs_s[:, t], at, order[:], ALU.is_gt, ALU.add
                                         ).then_inc(keep_done, 1)
                dve.wait_ge(keep_done, done(t))

            def split_gates(i, s):
                dve.wait_ge(hT_hi_done, done(2 * i + s))
                dve.tensor_tensor(hT_lo[:, s], hT_ps(s), hT_hi[:, s].bitcast(F32), ALU.subtract
                                  ).then_inc(hT_lo_done, 1)

            def norm(i, s):
                t = 2 * i + s
                dve.wait_ge(down_done, done(t))
                dve.wait_ge(x_in[s], landed(i))
                own.done(dve.tensor_tensor(y_sb[:, s], y_ps(s), x_sb[:, s], ALU.add))
                own.wait()
                own.done(dve.bn_stats(stats[:, s], y_sb[:, s]))
                own.wait_apart(dve_passed)
                own.done(dve.bn_aggr(mv[:, s], stats[:, s]))
                own.wait()
                dve.tensor_scalar(mv[:, s, 1:2], mv[:, s, 1:2], EPS, None, ALU.add).then_inc(mv_done, 1)
                dve.wait_ge(rstd_done, done(t))
                dve.wait_ge(x1_out[s], landed(i - 1))
                dve.wait_ge(x1T_done, done(t - 2))
                dve.tensor_scalar(x1_sb[:, s], y_sb[:, s], mv[:, s, 0:1], rstd[:, s:s + 1], ALU.subtract,
                                  ALU.mult).then_inc(x1_done, 1)

            def split_x1(i, s):
                t = 2 * i + s
                dve.wait_ge(x1T_hi_done, done(t))
                at = bass.ds(t * P, P)
                dve.tensor_tensor(x1T_lo[:, :, at], y_ps(s).rearrange("p (c n) -> p c n", c=CT),
                                  x1T_hi[:, :, at].bitcast(F32), ALU.subtract).then_inc(x1T_lo_done, 1)

            choose(0, 0)
            for n in range(IC):
                rows = P if n < IC - 1 else IR
                dve.wait_ge(w_hi_done, n + 1)
                dve.tensor_tensor(w_lo[0:rows, n], w_raw[0:rows, n % 2], w_hi[0:rows, n].bitcast(F32),
                                  ALU.subtract).then_inc(w_lo_done, 1)
            choose(0, 1)
            split_gates(0, 0)
            split_gates(0, 1)
            before = own.n
            with dve.Fori(0, TT // 2 - 1) as i:
                per_trip = 12
                own.base, own.n = before + per_trip * i, 0
                for s in range(2):
                    choose(i + 1, s)
                    norm(i, s)
                    split_x1(i, s)
                    split_gates(i + 1, s)
                assert own.n == per_trip
            own.base, own.n = before, per_trip * (TT // 2 - 1)
            for s in range(2):
                norm(TT // 2 - 1, s)
                split_x1(TT // 2 - 1, s)

        @block.tensor
        def _(pe):
            begin(pe, hT_done, down_done, x1T_done)
            pe.wait_ge(pads, 2)
            pe.wait_ge(w_pads, 2)

            def transpose_gates(i, s):
                pe.wait_ge(h_done, done(2 * i + s))
                pe.wait_ge(hT_lo_done, done(2 * i + s - 2))
                for c in range(IC):
                    last = pe.transpose(hT_ps(s)[:, c * P:(c + 1) * P], h_sb[:, s, c * P:(c + 1) * P], ident)
                last.then_inc(hT_done, 1)

            def down(i, s):
                pe.wait_ge(hT_lo_done, done(2 * i + s))
                pe.wait_ge(x1T_lo_done, done(2 * i + s - 2))
                for c in range(IC):
                    if isinstance(i, int) and (i, s) == (0, 0):
                        pe.wait_ge(w_lo_done, c + 1)
                    k = slice(c * P, (c + 1) * P)
                    last = product(pe, y_ps(s), hT_hi[:, s, k], hT_lo[:, s, k], w_hi[:, c], w_lo[:, c],
                                   c == 0, c == IC - 1)
                last.then_inc(down_done, 1)

            def transpose_x1(i, s):
                pe.wait_ge(x1_done, done(2 * i + s))
                for c in range(CT):
                    last = pe.transpose(y_ps(s)[:, c * P:(c + 1) * P], x1_sb[:, s, c * P:(c + 1) * P], ident)
                last.then_inc(x1T_done, 1)

            transpose_gates(0, 0)
            transpose_gates(0, 1)
            down(0, 0)
            with pe.Fori(0, TT // 2 - 1) as i:
                for s in range(2):
                    down(i + s, 1 - s)
                    transpose_gates(i + 1, s)
                    transpose_x1(i, s)
            down(TT // 2 - 1, 1)
            transpose_x1(TT // 2 - 1, 0)
            transpose_x1(TT // 2 - 1, 1)


def queries(nc, psum, ident, x1T_hi, x1T_lo, WqT, qn, kn, qS):
    with ExitStack() as ctx:
        def sb(name, shape, dt=F32):
            return ctx.enter_context(nc.sbuf_tensor(name, shape, dt))

        def sem(name):
            return ctx.enter_context(nc.semaphore(name))

        HG = H // G
        W = HG * HD
        BODY = 2 * TT
        TRIPS = G // 2
        LAG = 3
        w_raw = sb("wq_raw", [P, 2, CT, W])
        w_hi = sb("wq_hi", [P, 2, CT, W], F32R)
        w_lo = sb("wq_lo", [P, 2, CT, W], F32R)
        wn = sb("wn", [P, 2])
        w_qk = sb("w_qk", [P, 1])
        minus_half = sb("minus_half_q", [P, HG])
        square = sb("square_q", [P, 2, W])
        ssq = sb("ssq_q", [P, TT, HG])
        var = sb("var_q", [P, TT, HG])
        rstd = sb("rstd_q", [P, TT, HG])
        q_sb = sb("q_sb", [P, 4, W])
        qT_sb = sb("qT_sb", [P, 4, W])

        w_in = [sem(f"wq_in{s}") for s in range(2)]
        wn_in, half = sem("wn_in"), sem("half_q")
        w_hi_done, w_lo_done, w_qk_done = sem("wq_hi_done"), sem("wq_lo_done"), sem("w_qk_done")
        q_done, ssq_done, var_done, rstd_done = sem("q_done"), sem("ssq_q"), sem("var_done_q"), sem("rstd_done_q")
        q_sb_done, qT_done, qT_sb_done = sem("q_sb_done"), sem("qT_done"), sem("qT_sb_done")
        qT_out = [sem(f"qT_out{s}") for s in range(4)]

        def steps(eng, step, ahead=0):
            with eng.Fori(0, TRIPS - 1) as i:
                for s in range(BODY):
                    step(i, s)
            for s in range(BODY):
                step(TRIPS - 1, s)

        def last_trip(i):
            return isinstance(i, int) and i == TRIPS - 1

        block = ctx.enter_context(nc.Block())

        @block.sync
        def _(sp):
            begin_dma(sp, *w_in, *qT_out)
            sp.dma_start(wn[:, 0:1], qn).then_inc(wn_in, 16)
            sp.dma_start(wn[:, 1:2], kn).then_inc(wn_in, 16)

            def load_w(i, r):
                sp.wait_ge(w_lo_done, done(2 * i + r - 2))
                sp.dma_start(w_raw[:, r], cols(WqT)[:, :, bass.ds((2 * i + r) * W, W)]).then_inc(w_in[r], 16)

            def step(i, s):
                if s % TT == 0 and not last_trip(i):
                    load_w(i + 1, s // TT)
                sp.wait_ge(qT_sb_done, done(BODY * i + s))
                t, b = s % TT, s % TT // (S // P)
                at = slice((t - b * (S // P)) * P, (t - b * (S // P) + 1) * P)
                sp.dma_start(qS[b, 2 * i + s // TT, :, :, at], qT_sb[:, s % 4].rearrange("d (h q) -> d h q", h=HG)
                             ).then_inc(qT_out[s % 4], 16)

            load_w(0, 0)
            load_w(0, 1)
            steps(sp, step)
            for s in range(4):
                sp.wait_ge(qT_out[s], landed(BODY * TRIPS // 4 - 1))

        @block.gpsimd
        def _(pool):
            begin(pool, rstd_done)
            pool.memset(minus_half[:], -0.5).then_inc(half, 1)
            pool.wait_ge(half, 1)

            def step(i, s):
                pool.wait_ge(var_done, done(BODY * i + s))
                pool.tensor_tensor(rstd[:, s % TT], var[:, s % TT], minus_half[:], ALU.pow).then_inc(rstd_done, 1)

            steps(pool, step)

        @block.scalar
        def _(act):
            begin(act, w_hi_done, ssq_done, qT_sb_done)
            act.wait_ge(w_qk_done, 1)

            def split_w(i, r):
                act.wait_ge(w_in[r], landed(i))
                act.wait_ge(q_done, done(BODY * i + TT * (r + 1) - 1 - BODY))
                act.copy(w_hi[:, r], w_raw[:, r]).then_inc(w_hi_done, 1)

            def squares(i, s):
                n = BODY * i + s
                act.wait_ge(q_done, done(n))
                act.wait_ge(ssq_done, done(n - 2))
                for h in range(HG):
                    last = act.activation(square[:, s % 2, h * HD:(h + 1) * HD], psum[:, s % TT, h * HD:(h + 1) * HD],
                                          ACT.Square, accum_out=ssq[:, s % TT, h:h + 1])
                last.then_inc(ssq_done, 1)

            def step(i, s):
                n = BODY * i + s
                if not (last_trip(i) and s + LAG >= BODY):
                    squares(i, s + LAG)
                act.wait_ge(qT_done, done(n))
                act.wait_ge(qT_out[s % 4], landed(BODY // 4 * i + s // 4 - 1))
                act.mul(qT_sb[:, s % 4], psum[:, s % TT], w_qk[:, 0:1]).then_inc(qT_sb_done, 1)
                if s % TT == 0 and not (last_trip(i) and s):
                    split_w(i + s // TT, 1 - s // TT)

            split_w(0, 0)
            for s in range(LAG):
                squares(0, s)
            steps(act, step)

        @block.vector
        def _(dve):
            begin(dve, w_lo_done, var_done, q_sb_done)
            dve.wait_ge(wn_in, 32)
            dve.scalar_tensor_tensor(w_qk[:], wn[:, 0:1], -float(HD) ** -0.5, wn[:, 1:2], ALU.mult, ALU.mult
                                     ).then_inc(w_qk_done, 1)

            def split_w(i, r):
                dve.wait_ge(w_hi_done, done(2 * i + r))
                dve.tensor_tensor(w_lo[:, r], w_raw[:, r], w_hi[:, r].bitcast(F32), ALU.subtract
                                  ).then_inc(w_lo_done, 1)

            def variance(i, s):
                dve.wait_ge(ssq_done, done(BODY * i + s))
                dve.tensor_scalar(var[:, s % TT], ssq[:, s % TT], 1.0 / HD, EPS, ALU.mult, ALU.add
                                  ).then_inc(var_done, 1)

            def norm(i, s):
                n = BODY * i + s
                dve.wait_ge(rstd_done, done(n))
                dve.wait_ge(qT_done, done(n - 4))
                dve.tensor_tensor(q_sb[:, s % 4].rearrange("p (h d) -> p h d", h=HG),
                                  psum[:, s % TT].rearrange("p (h d) -> p h d", h=HG),
                                  rstd[:, s % TT].unsqueeze(2).to_broadcast((P, HG, HD)), ALU.mult
                                  ).then_inc(q_sb_done, 1)

            def step(i, s):
                if not (last_trip(i) and s + 2 >= BODY):
                    variance(i, s + 2)
                norm(i, s)
                if s % TT == 0 and not (last_trip(i) and s):
                    split_w(i + s // TT, 1 - s // TT)

            split_w(0, 0)
            variance(0, 0)
            variance(0, 1)
            steps(dve, step)

        @block.tensor
        def _(pe):
            begin(pe, q_done, qT_done)

            def project(i, s):
                i, s = (i + 1, s - BODY) if s >= BODY else (i, s)
                r, t = s // TT, s % TT
                pe.wait_ge(w_lo_done, done(2 * i + r))
                pe.wait_ge(qT_sb_done, done(BODY * i + s - TT))
                for c in range(CT):
                    at = slice(t * P, (t + 1) * P)
                    last = product(pe, psum[:, t], x1T_hi[:, c, at], x1T_lo[:, c, at], w_hi[:, r, c], w_lo[:, r, c],
                                   c == 0, c == CT - 1)
                last.then_inc(q_done, 1)

            def step(i, s):
                if not (last_trip(i) and s + LAG >= BODY):
                    project(i, s + LAG)
                pe.wait_ge(q_sb_done, done(BODY * i + s))
                for h in range(HG):
                    last = pe.transpose(psum[:, s % TT, h * P:(h + 1) * P], q_sb[:, s % 4, h * HD:(h + 1) * HD], ident)
                last.then_inc(qT_done, 1)

            for s in range(LAG):
                project(0, s)
            steps(pe, step)


def attention(nc, psum, ident, mask, qS, kS, vS, oS):
    with ExitStack() as ctx:
        def sb(name, shape, dt=F32):
            return ctx.enter_context(nc.sbuf_tensor(name, shape, dt))

        def sem(name):
            return ctx.enter_context(nc.semaphore(name))

        ITEMS = B * G
        UNITS = 2 * ITEMS
        QT = 4
        QW = QT * P
        SB, SW = 4, 402
        KP = SB * SW
        NT = (KV + P - 1) // P
        KR = KV - (NT - 1) * P
        LAG = 3
        TB = 3
        RING = 4
        BODY = 4
        TRIPS = UNITS // BODY
        AT = {0: 1, 2: 2, 5: 3, 10: 0}
        INVERT_AT = {0: 0, 3: 1, 5: 2, 8: 3}
        assert NT * BODY % RING == 0 and KP >= KV + KV % 2

        q_raw = sb("q_raw", [P, 2 * QW])
        k_raw = sb("k_raw", [P, KP])
        v_raw = sb("v_raw", [P, NT * HD])
        q_hi = sb("q_hi", [P, 2, 2 * QW], F32R)
        q_lo = sb("q_lo", [P, 2, 2 * QW], F32R)
        k_hi = sb("k_hi", [P, 2, KP], F32R)
        k_lo = sb("k_lo", [P, 2, KP], F32R)
        v_hi = sb("v_hi", [P, 2, NT * HD], F32R)
        v_lo = sb("v_lo", [P, 2, NT * HD], F32R)
        minus_mask = sb("minus_mask", [P, S // P, KP])
        p_sb = sb("p_sb_a", [P, 2, QT, KP])
        t_min = sb("t_min", [P, 2 * QT])
        p_sum = sb("p_sum", [P, 2 * QT])
        p_inv = sb("p_inv", [P, 2 * QT])
        pT_hi = sb("pT_hi", [P, RING, QW], F32R)
        pT_lo = sb("pT_lo", [P, RING, QW], F32R)
        o_sb = sb("o_sb", [P, 2, QW])

        def t_bank(m):
            return psum[:, SB + m % (NT * BODY) % TB, :]

        mask_in, k_in, q_in, v_in = sem("mask_in"), sem("k_in"), sem("q_in"), sem("v_in")
        pads, mask_done = sem("pads_a"), sem("mask_done")
        kq_hi, kq_lo = sem("kq_hi"), sem("kq_lo")
        v_hi_done, v_lo_done = sem("v_hi_done"), sem("v_lo_done")
        s_done = sem("s_done_a")
        t_done, e_done, inv_done, p_done = sem("t_done"), sem("e_done"), sem("inv_done"), sem("p_done_a")
        pT_done, pT_hi_done, pT_lo_done = sem("pT_done"), sem("pT_hi_done"), sem("pT_lo_done")
        pv_done = sem("pv_done")
        o_done = sem("o_done")
        o_out = [sem(f"o_out{s}") for s in range(2)]
        pool_passed, dve_passed = sem("pool_passed_a"), sem("dve_passed_a")

        s_ps = psum[:, 0:SB, 0:SW]
        o_ps = psum[:, SB + TB, :]

        def banked(ap):
            return ap.rearrange("p (b n) -> p b n", b=SB)

        def rows(kt):
            return P if kt < NT - 1 else KR

        def schedule(eng, position):
            with eng.Fori(0, TRIPS - 1) as i:
                for u in range(BODY):
                    for kt in range(NT):
                        position(i, u, kt)
            for u in range(BODY):
                for kt in range(NT):
                    position(TRIPS - 1, u, kt)

        def last_trip(i):
            return isinstance(i, int) and i == TRIPS - 1

        def exists(i, u):
            return u < BODY or not last_trip(i)

        def scored(u, kt):
            return (u + 1, AT[kt]) if AT[kt] else (u + 2, 0)

        def transposed(u, kt):
            return (u, kt + LAG) if kt + LAG < NT else (u + 1, kt + LAG - NT)

        def tile(i, u, j):
            return QT * (BODY * i + u) + j

        def key_step(i, u, kt):
            return NT * (BODY * i + u) + kt

        KQ = [(k_raw, k_hi, k_lo, slice(0, KP // 2)), (k_raw, k_hi, k_lo, slice(KP // 2, KP)),
              (q_raw, q_hi, q_lo, slice(0, 2 * QW))]
        V = [(v_raw, v_hi, v_lo, slice(0, NT * HD // 2)), (v_raw, v_hi, v_lo, slice(NT * HD // 2, NT * HD))]
        SPLIT_AT = {1: 0, 4: 1, 7: 2}

        def splits(i, u, kt, kq, v):
            if kt not in SPLIT_AT:
                return
            if u % 2 and not last_trip(i):
                kq(2 * i + u // 2 + 2, u // 2 % 2, SPLIT_AT[kt])
            if not u % 2 and SPLIT_AT[kt] < len(V) and not (last_trip(i) and u):
                v(2 * i + u // 2 + 1, (u // 2 + 1) % 2, SPLIT_AT[kt])

        block = ctx.enter_context(nc.Block())

        @block.sync
        def _(sp):
            begin_dma(sp, k_in, q_in, v_in, *o_out)

            def load_kq(item):
                sp.wait_ge(kq_lo, done(len(KQ) * item - 1))
                sp.dma_start(k_raw[:, 0:KV], kS[item % G, :, bass.ds(item // G * KV, KV)]).then_inc(k_in, 16)
                sp.dma_start(q_raw[:], qS[item]).then_inc(q_in, 16)

            def load_v(item):
                sp.wait_ge(v_lo_done, done(len(V) * item - 1))
                at = bass.ds(item % G * HD, HD)
                sp.dma_start(v_raw[:, 0:(NT - 1) * HD].rearrange("p (t d) -> p t d", d=HD),
                             vS[bass.ds(item // G * KV, KV - KR), at].rearrange("(t p) d -> p t d", p=P)
                             ).then_inc(v_in, 16)
                sp.dma_start(v_raw[0:KR, (NT - 1) * HD:NT * HD],
                             vS[bass.ds(item // G * KV + (KV - KR), KR), at]).then_inc(v_in, 16)

            def position(i, u, kt):
                if kt == 1 and not last_trip(i):
                    if u % 2:
                        load_v(2 * i + u // 2 + 2)
                    else:
                        load_kq(2 * i + u // 2 + 2)
                if kt == NT - 1:
                    sp.wait_ge(o_done, done(BODY * i + u))
                    sp.dma_start(oS[BODY * i + u], o_sb[:, u % 2]).then_inc(o_out[u % 2], 16)

            load_kq(0)
            for r in range(S // P):
                sp.dma_start(minus_mask[:, r, 0:KV], mask[r * P:(r + 1) * P, :]).then_inc(mask_in, 16)
            sp.wait_ge(pads, 3)
            load_v(0)
            load_kq(1)
            load_v(1)
            schedule(sp, position)
            for s in range(2):
                sp.wait_ge(o_out[s], landed(UNITS // 2 - 1))

        @block.gpsimd
        def _(pool):
            begin(pool, kq_lo, v_lo_done, p_done)
            pool.memset(k_raw[:, KV:KP], 0.0).then_inc(pads, 1)
            pool.wait_ge(pads, 1)
            pool.memset(minus_mask[:, :, KV:KP], 3.4028235e38).then_inc(pads, 1)
            pool.wait_ge(pads, 2)
            pool.memset(v_raw[P // 2:P, (NT - 1) * HD:NT * HD], 0.0).then_inc(pads, 1)
            pool.wait_ge(pads, 3)

            def split(hi_done, lo_done, parts):
                def do(item, slot, n):
                    raw, hi, lo, at = parts[n]
                    pool.wait_ge(hi_done, done(len(parts) * item + n))
                    pool.tensor_tensor(lo[:, slot, at], raw[:, at], hi[:, slot, at].bitcast(F32), ALU.subtract
                                       ).then_inc(lo_done, 1)
                return do

            split_kq, split_v = split(kq_hi, kq_lo, KQ), split(v_hi_done, v_lo_done, V)

            def norm(i, u, j):
                at = p_sb[:, u % 2, j, 0:KV]
                wait_apart(pool, inv_done, done(tile(i, u, j)), pool_passed)
                n = QT * (u % 2) + j
                pool.tensor_scalar(at, at, p_inv[:, n:n + 1], 1.0, ALU.mult, ALU.mult).then_inc(p_done, 1)

            def position(i, u, kt):
                if kt in INVERT_AT and exists(i, u + 1):
                    norm(i, u + 1, INVERT_AT[kt])
                splits(i, u, kt, split_kq, split_v)

            for n in range(len(KQ)):
                split_kq(0, 0, n)
            for j in range(QT):
                norm(0, 0, j)
            for n in range(len(V)):
                split_v(0, 0, n)
            for n in range(len(KQ)):
                split_kq(1, 1, n)
            schedule(pool, position)

        @block.scalar
        def _(act):
            begin(act, kq_hi, v_hi_done, e_done, pT_hi_done, o_done)
            act.wait_ge(pads, 3)

            def split_kq(item, slot, n):
                raw, hi, _, at = KQ[n]
                act.wait_ge(k_in if n < 2 else q_in, landed(item))
                act.wait_ge(s_done, done(QT * 2 * (item - 1) - 1))
                act.copy(hi[:, slot, at], raw[:, at]).then_inc(kq_hi, 1)

            def split_v(item, slot, n):
                raw, hi, _, at = V[n]
                act.wait_ge(v_in, landed(2 * item + 1))
                act.wait_ge(pv_done, done(NT * 2 * (item - 1) - 1))
                act.copy(hi[:, slot, at], raw[:, at]).then_inc(v_hi_done, 1)

            def exp(i, u, j):
                n = QT * (u % 2) + j
                at = p_sb[:, u % 2, j, 0:KV]
                act.wait_ge(t_done, done(tile(i, u, j)))
                act.activation(at, at, ACT.Exp, bias=t_min[:, n:n + 1], scale=-1.0, accum_out=p_sum[:, n:n + 1]
                               ).then_inc(e_done, 1)

            def split_p(i, u, kt):
                m, n = NT * u + kt, key_step(i, u, kt)
                act.wait_ge(pT_done, done(n))
                act.wait_ge(pv_done, done(n - RING))
                act.copy(pT_hi[0:rows(kt), m % RING], t_bank(m)[0:rows(kt)]).then_inc(pT_hi_done, 1)

            def position(i, u, kt):
                if exists(i, transposed(u, kt)[0]):
                    split_p(i, *transposed(u, kt))
                if kt == NT - 1:
                    act.wait_ge(pv_done, done(key_step(i, u, kt)))
                    act.wait_ge(o_out[u % 2], landed(BODY // 2 * i + u // 2 - 1))
                    act.copy(o_sb[:, u % 2], o_ps).then_inc(o_done, 1)
                if kt in AT and exists(i, scored(u, kt)[0]):
                    exp(i, *scored(u, kt))
                splits(i, u, kt, split_kq, split_v)

            for n in range(len(KQ)):
                split_kq(0, 0, n)
            for j in range(QT):
                exp(0, 0, j)
            for n in range(len(V)):
                split_v(0, 0, n)
            for n in range(len(KQ)):
                split_kq(1, 1, n)
            exp(0, 1, 0)
            for kt in range(LAG):
                split_p(0, 0, kt)
            schedule(act, position)

        @block.vector
        def _(dve):
            begin(dve, t_done, inv_done, pT_lo_done)
            dve.wait_ge(mask_in, 16 * (S // P))
            dve.tensor_scalar(minus_mask[:, :, 0:KV], minus_mask[:, :, 0:KV], -1.0, None, ALU.mult
                              ).then_inc(mask_done, 1)
            dve.wait_ge(mask_done, 1)
            dve.wait_ge(pads, 2)

            def subtract_mask(i, u, j):
                n = QT * (u % 2) + j
                wait_apart(dve, s_done, done(tile(i, u, j)), dve_passed)
                dve.tensor_tensor_reduce(banked(p_sb[:, u % 2, j]), s_ps, banked(minus_mask[:, j % 2]), 1.0,
                                         3.4028235e38, ALU.add, ALU.min, t_min[:, n:n + 1]).then_inc(t_done, 1)

            def invert(i, u, j):
                n = QT * (u % 2) + j
                dve.wait_ge(e_done, done(tile(i, u, j)))
                dve.reciprocal(p_inv[:, n:n + 1], p_sum[:, n:n + 1]).then_inc(inv_done, 1)

            def split_p(i, u, kt):
                m, n = NT * u + kt, key_step(i, u, kt)
                dve.wait_ge(pT_hi_done, done(n))
                dve.tensor_tensor(pT_lo[0:rows(kt), m % RING], t_bank(m)[0:rows(kt)],
                                  pT_hi[0:rows(kt), m % RING].bitcast(F32), ALU.subtract).then_inc(pT_lo_done, 1)

            def position(i, u, kt):
                if kt in INVERT_AT and exists(i, u + 1):
                    invert(i, u + 1, INVERT_AT[kt])
                if kt in AT and exists(i, scored(u, kt)[0]):
                    subtract_mask(i, *scored(u, kt))
                if exists(i, transposed(u, kt)[0]):
                    split_p(i, *transposed(u, kt))

            subtract_mask(0, 0, 0)
            for j in range(1, QT):
                subtract_mask(0, 0, j)
                invert(0, 0, j - 1)
            invert(0, 0, QT - 1)
            subtract_mask(0, 1, 0)
            for kt in range(LAG):
                split_p(0, 0, kt)
            schedule(dve, position)

        @block.tensor
        def _(pe):
            begin(pe, s_done, pT_done, pv_done)

            def score(i, u, j):
                slot, q = u // 2 % 2, slice(QW * (u % 2) + P * j, QW * (u % 2) + P * (j + 1))
                if j == 0 and u % 2 == 0:
                    pe.wait_ge(kq_lo, done(len(KQ) * (2 * i + u // 2 + 1) - 1))
                pe.wait_ge(t_done, done(tile(i, u, j) - 1))
                for b in range(SB):
                    k = slice(SW * b, SW * (b + 1))
                    last = product(pe, psum[:, b, 0:SW], q_hi[:, slot, q], q_lo[:, slot, q],
                                   k_hi[:, slot, k], k_lo[:, slot, k], True, True)
                last.then_inc(s_done, 1)

            def transpose_p(i, u, kt):
                m, n = NT * u + kt, key_step(i, u, kt)
                if kt == 0:
                    pe.wait_ge(p_done, done(tile(i, u, QT - 1)))
                pe.wait_ge(pT_lo_done, done(n - 1 if m % (NT * BODY) == 0 else n - TB))
                for j in range(QT):
                    last = pe.transpose(t_bank(m)[0:rows(kt), P * j:P * (j + 1)],
                                        p_sb[:, u % 2, j, P * kt:P * kt + rows(kt)], ident)
                last.then_inc(pT_done, 1)

            def weigh_values(i, u, kt):
                m, n, slot = NT * u + kt, key_step(i, u, kt), u // 2 % 2
                r, d = rows(kt), slice(HD * kt, HD * (kt + 1))
                if kt == 0:
                    pe.wait_ge(v_lo_done, done(len(V) * (2 * i + u // 2 + 1) - 1))
                    pe.wait_ge(o_done, done(BODY * i + u - 1))
                pe.wait_ge(pT_lo_done, done(n))
                product(pe, o_ps, v_hi[0:r, slot, d], v_lo[0:r, slot, d], pT_hi[0:r, m % RING], pT_lo[0:r, m % RING],
                        kt == 0, kt == NT - 1).then_inc(pv_done, 1)

            def position(i, u, kt):
                if kt in AT and exists(i, scored(u, kt)[0]):
                    score(i, *scored(u, kt))
                weigh_values(i, u, kt)
                if exists(i, transposed(u, kt)[0]):
                    transpose_p(i, *transposed(u, kt))

            for j in range(QT):
                score(0, 0, j)
            score(0, 1, 0)
            for kt in range(LAG):
                transpose_p(0, 0, kt)
            schedule(pe, position)


def output_and_experts(nc, psum, ident, oS, WoT, x1S, AT, routeT, BwT, out):
    with ExitStack() as ctx:
        def sb(name, shape, dt=F32):
            return ctx.enter_context(nc.sbuf_tensor(name, shape, dt))

        def sem(name):
            return ctx.enter_context(nc.semaphore(name))

        PAIRS = H // 2
        W = 2 * S
        PIECES = B + 1
        o_raw = sb("o_raw", [P, 2, B, W])
        o_hi = sb("o_hi", [P, 2, B, W], F32R)
        o_lo = sb("o_lo", [P, 2, B, W], F32R)
        w_raw = sb("wo_raw", [P, 2, 2, D])
        w_hi = sb("wo_hi", [P, 2, 2, D], F32R)
        w_lo = sb("wo_lo", [P, 2, 2, D], F32R)
        x1_sb = sb("x1_in", [P, TT, D])
        expert_in = sb("expert_in", [P, CT, E * R + E])
        expert_out = sb("expert_out", [P, D])
        y_sb = sb("y_sb", [P, TT, D])
        stats = sb("stats", [P, TT, 6])
        mv = sb("mv", [P, TT, 2])
        rstd = sb("rstd_f", [P, TT])
        minus_half = sb("minus_half_f", [P, 1])
        x2_sb = sb("x2_sb", [P, TT, D])
        x2T_sb = sb("x2T_sb", [P, TT, D])
        rank = sb("rank", [P, E])
        best = sb("best", [P, TT])
        ranked = sb("ranked", [P, TT, E])
        first = sb("first", [P, TT])
        route = sb("route", [P, TT, E])
        wh_sb = sb("wh_sb", [P, TT, E * R])
        whT_sb = sb("whT_sb", [P, TT, P])
        out_sb = sb("out_sb", [P, TT, D])

        o_in = [sem(f"o_in{s}") for s in range(2)]
        w_in = [sem(f"wo_in{s}") for s in range(2)]
        x1_in, expert_loaded, consts = sem("x1_in_done"), sem("expert_loaded"), sem("consts")
        hi_done, lo_done = sem("hi_done_f"), sem("lo_done_f")
        pair_done = sem("pair_done")
        sum_done = sem("sum_done")
        chain, mv_done, rstd_done, x2_done = sem("chain_f"), sem("mv_done_f"), sem("rstd_done_f"), sem("x2_done")
        x2T_done, x2T_sb_done, h_done, wh_done = sem("x2T_done"), sem("x2T_sb_done"), sem("h_done_f"), sem("wh_done")
        whT_done, whT_sb_done, f_done = sem("whT_done"), sem("whT_sb_done"), sem("f_done")
        out_done, out_out = sem("out_done"), sem("out_out")

        o_view = oS.rearrange("(b h) d n -> h d b n", b=B)

        def pairs(eng, step):
            step(0, 0, True, False)
            with eng.Fori(0, PAIRS // 2 - 1) as i:
                step(i, 1, False, False)
                step(i + 1, 0, False, False)
            step(PAIRS // 2 - 1, 1, False, True)

        def bank(t):
            return psum[:, t, :]

        block = ctx.enter_context(nc.Block())

        @block.sync
        def _(sp):
            begin_dma(sp, *o_in, *w_in)

            def load(i, r, *_):
                sp.wait_ge(lo_done, done(PIECES * (2 * i + r - 1) - 1))
                sp.dma_start(w_raw[:, r], cols(WoT)[:, bass.ds(2 * (2 * i + r), 2), :]).then_inc(w_in[r], 16)
                sp.dma_start(o_raw[:, r], o_view[2 * i + r]).then_inc(o_in[r], 16)

            pairs(sp, load)
            sp.dma_start(x1_sb[:], cols(x1S)).then_inc(x1_in, 16)
            sp.dma_start(expert_in[:, :, 0:E * R], cols(AT)).then_inc(expert_loaded, 16)
            sp.dma_start(expert_in[:, :, E * R:E * R + E], cols(routeT)).then_inc(expert_loaded, 16)
            sp.dma_start(expert_out[:], BwT).then_inc(expert_loaded, 16)

            for s in range(TT):
                sp.wait_ge(out_done, done(s))
                sp.dma_start(out[s * P:(s + 1) * P, :], out_sb[:, s]).then_inc(out_out, 16)

            sp.wait_ge(out_out, 16 * TT)

        @block.gpsimd
        def _(pool):
            begin(pool, rstd_done)
            pool.memset(minus_half[:], -0.5).then_inc(consts, 1)
            for e in range(E):
                pool.memset(rank[:, e:e + 1], float(E - e)).then_inc(consts, 1)
            pool.wait_ge(consts, 1)

            for norm in range(2):
                for s in range(TT):
                    n = TT * norm + s
                    pool.wait_ge(mv_done, done(n))
                    pool.tensor_tensor(rstd[:, s:s + 1], mv[:, s, 1:2], minus_half[:], ALU.pow
                                       ).then_inc(rstd_done, 1)

        @block.scalar
        def _(act):
            begin(act, hi_done, x2T_sb_done, whT_sb_done)

            def split(i, r, *_):
                act.wait_ge(w_in[r], landed(i))
                act.wait_ge(pair_done, done(2 * i + r - 2))
                act.copy(w_hi[:, r], w_raw[:, r]).then_inc(hi_done, 1)
                act.wait_ge(o_in[r], landed(i))
                for b in range(B):
                    act.copy(o_hi[:, r, b], o_raw[:, r, b]).then_inc(hi_done, 1)

            pairs(act, split)

            for s in range(TT):
                act.wait_ge(x2T_done, done(s))
                act.copy(x2T_sb[:, s], bank(s)).then_inc(x2T_sb_done, 1)
            for s in range(TT):
                act.wait_ge(whT_done, done(s))
                act.copy(whT_sb[:, s], bank(s)[:, 0:P]).then_inc(whT_sb_done, 1)

        @block.vector
        def _(dve):
            begin(dve, lo_done, mv_done, x2_done, wh_done, out_done)

            def split(i, r, *_):
                n = PIECES * (2 * i + r)
                dve.wait_ge(hi_done, done(n))
                dve.tensor_tensor(w_lo[:, r], w_raw[:, r], w_hi[:, r].bitcast(F32), ALU.subtract
                                  ).then_inc(lo_done, 1)
                for b in range(B):
                    dve.wait_ge(hi_done, done(n + 1 + b))
                    dve.tensor_tensor(o_lo[:, r, b], o_raw[:, r, b], o_hi[:, r, b].bitcast(F32), ALU.subtract
                                      ).then_inc(lo_done, 1)

            pairs(dve, split)
            dve.wait_ge(x1_in, 16)
            dve.wait_ge(consts, 1 + E)
            own = Chain(dve, chain)

            def moments(s, increase, x):
                own.done(dve.tensor_tensor(y_sb[:, s], increase, x, ALU.add))
                own.wait()
                own.done(dve.bn_stats(stats[:, s], y_sb[:, s]))
                own.wait()
                own.done(dve.bn_aggr(mv[:, s], stats[:, s]))
                own.wait()
                dve.tensor_scalar(mv[:, s, 1:2], mv[:, s, 1:2], EPS, None, ALU.add).then_inc(mv_done, 1)

            def norm(n, s, to, ready):
                dve.wait_ge(rstd_done, done(n))
                dve.tensor_scalar(to, y_sb[:, s], mv[:, s, 0:1], rstd[:, s:s + 1], ALU.subtract, ALU.mult
                                  ).then_inc(ready, 1)

            def weigh(s):
                logits = bank(s)[:, E * R:E * R + E]
                dve.wait_ge(h_done, done(s))
                own.done(dve.tensor_reduce(best[:, s:s + 1], logits, mybir.AxisListType.X, ALU.max))
                own.wait()
                own.done(dve.scalar_tensor_tensor(ranked[:, s], logits, best[:, s:s + 1], rank[:], ALU.is_equal,
                                                  ALU.mult))
                own.wait()
                own.done(dve.tensor_reduce(first[:, s:s + 1], ranked[:, s], mybir.AxisListType.X, ALU.max))
                own.wait()
                own.done(dve.tensor_scalar(route[:, s], ranked[:, s], first[:, s:s + 1], best[:, s:s + 1],
                                           ALU.is_equal, ALU.mult))
                own.wait()
                dve.tensor_tensor(wh_sb[:, s].rearrange("p (e r) -> p e r", e=E),
                                  bank(s)[:, 0:E * R].rearrange("p (e r) -> p e r", e=E),
                                  route[:, s].unsqueeze(2).to_broadcast((P, E, R)), ALU.mult).then_inc(wh_done, 1)

            for s in range(TT):
                dve.wait_ge(sum_done, done(s))
                moments(s, bank(s), x1_sb[:, s])
                if s:
                    norm(s - 1, s - 1, x2_sb[:, s - 1], x2_done)
            norm(TT - 1, TT - 1, x2_sb[:, TT - 1], x2_done)
            for s in range(TT):
                weigh(s)
            for s in range(TT):
                dve.wait_ge(f_done, done(s))
                moments(s, bank(s), x2_sb[:, s])
                if s:
                    norm(TT + s - 1, s - 1, out_sb[:, s - 1], out_done)
            norm(2 * TT - 1, TT - 1, out_sb[:, TT - 1], out_done)

        @block.tensor
        def _(pe):
            begin(pe, pair_done, sum_done, x2T_done, h_done, whT_done, f_done)

            def multiply(i, r, start, stop):
                for b in range(B):
                    pe.wait_ge(lo_done, done(PIECES * (2 * i + r) + 1 + b))
                    for j in range(S // P):
                        for h in range(2):
                            q = slice(h * S + j * P, h * S + (j + 1) * P)
                            last = product(pe, psum[:, b * (S // P) + j, :], o_hi[:, r, b, q], o_lo[:, r, b, q],
                                           w_hi[:, r, h], w_lo[:, r, h], start and h == 0, stop and h == 1)
                        if stop:
                            last.then_inc(sum_done, 1)
                if not stop:
                    last.then_inc(pair_done, 1)

            pairs(pe, multiply)
            pe.wait_ge(expert_loaded, 48)

            for s in range(TT):
                pe.wait_ge(x2_done, done(s))
                for c in range(CT):
                    last = pe.transpose(bank(s)[:, c * P:(c + 1) * P], x2_sb[:, s, c * P:(c + 1) * P], ident)
                last.then_inc(x2T_done, 1)
            for s in range(TT):
                pe.wait_ge(x2T_sb_done, done(s))
                for c in range(CT):
                    last = pe.matmul(bank(s)[:, 0:E * R + E], x2T_sb[:, s, c * P:(c + 1) * P],
                                     expert_in[:, c], start=c == 0, stop=c == CT - 1)
                last.then_inc(h_done, 1)
            for s in range(TT):
                pe.wait_ge(wh_done, done(s))
                pe.transpose(bank(s)[:, 0:P], wh_sb[:, s], ident).then_inc(whT_done, 1)
            for s in range(TT):
                pe.wait_ge(whT_sb_done, done(s))
                pe.matmul(bank(s), whT_sb[:, s], expert_out[:], start=True, stop=True).then_inc(f_done, 1)



def decoder_layer(nc, x, xT, ctxT, mask, WgT, WuT, WdT, WqT, WkT, WvT, WoT, qn, kn, routeT, AT, BwT, out):
    pS = nc.dram_tensor("gated_products", (TT, P, I), F32).ap()
    kS = nc.dram_tensor("keys", (G, HD, NK), F32).ap()
    vS = nc.dram_tensor("values", (NK, G * HD), F32).ap()
    x1S = nc.dram_tensor("x1", (T, D), F32).ap()
    qS = nc.dram_tensor("queries", (B, G, HD, H // G, S), F32).ap()
    oS = nc.dram_tensor("attended", (B * H // 2, HD, 2 * S), F32).ap()
    with ExitStack() as ctx:
        psum = ctx.enter_context(nc.psum_tensor("banks", [P, 8, 512], F32))
        ident = ctx.enter_context(nc.sbuf_tensor("ident", [P, P], F32))
        make_identity(nc, ident[:])
        abs_s = ctx.enter_context(nc.sbuf_tensor("abs_s", [P, TT, I], F32))
        thr = ctx.enter_context(nc.sbuf_tensor("thr", [P, TT], U32))
        n_less = ctx.enter_context(nc.sbuf_tensor("n_less", [P, TT], F32))
        gate_and_up(nc, psum, abs_s, xT, WgT, WuT, pS)
        keys_and_values(nc, psum, ident[:], abs_s, thr, n_less, ctxT, WkT, WvT, kS, vS)
        x1T_hi = ctx.enter_context(nc.sbuf_tensor("x1T_hi", [P, CT, T], F32R))
        x1T_lo = ctx.enter_context(nc.sbuf_tensor("x1T_lo", [P, CT, T], F32R))
        down_and_norm(nc, psum, ident[:], abs_s, thr, n_less, x1T_hi, x1T_lo, x, WdT, pS, x1S)
        queries(nc, psum, ident[:], x1T_hi, x1T_lo, WqT, qn, kn, qS)
    with ExitStack() as ctx:
        psum = ctx.enter_context(nc.psum_tensor("banks_2", [P, 8, 512], F32))
        ident = ctx.enter_context(nc.sbuf_tensor("ident_2", [P, P], F32))
        make_identity(nc, ident[:])
        attention(nc, psum, ident[:], mask, qS.rearrange("b g d h q -> (b g) d (h q)"), kS, vS, oS)
        output_and_experts(nc, psum, ident[:], oS, WoT, x1S, AT, routeT, BwT, out)


def kernel(x, ctx_4096, mask_1x1xSxS2_ff0, L0_attn_w_gate, L0_attn_w_up, L0_attn_w_down, L0_xattn_Wq, L0_xattn_Wk,
           L0_xattn_Wv, L0_xattn_Wo, L0_xattn_q_norm_w, L0_xattn_k_norm_w, L0_ffn_route_w, L0_ffn_A, L0_ffn_Bw):
    import numpy as np
    import concourse.bacc as bacc
    from concourse.bass_utils import run_bass_kernel_spmd

    def transposed(a, rows):
        return np.ascontiguousarray(np.asarray(a).reshape(rows, -1).T)

    x = np.asarray(x).reshape(T, D)
    arrays = {
        "x": np.ascontiguousarray(x),
        "xT": transposed(x, T),
        "ctxT": transposed(ctx_4096, NK),
        "mask": np.ascontiguousarray(np.asarray(mask_1x1xSxS2_ff0).reshape(S, KV)),
        "WgT": transposed(L0_attn_w_gate, I),
        "WuT": transposed(L0_attn_w_up, I),
        "WdT": transposed(L0_attn_w_down, D),
        "WqT": transposed(L0_xattn_Wq, H * HD),
        "WkT": transposed(L0_xattn_Wk, G * HD),
        "WvT": transposed(L0_xattn_Wv, G * HD),
        "WoT": transposed(L0_xattn_Wo, D),
        "qn": np.ascontiguousarray(np.asarray(L0_xattn_q_norm_w).reshape(HD, 1)),
        "kn": np.ascontiguousarray(np.asarray(L0_xattn_k_norm_w).reshape(HD, 1)),
        "routeT": transposed(L0_ffn_route_w, E),
        "AT": transposed(L0_ffn_A, E * R),
        "BwT": np.ascontiguousarray(np.asarray(L0_ffn_Bw).transpose(0, 2, 1).reshape(E * R, D)),
    }
    nc = bacc.Bacc("TRN2", target_bir_lowering=False, num_devices=1)
    args = {name: nc.dram_tensor(name + "_in", a.shape, mybir.dt.from_np(a.dtype), kind="ExternalInput").ap()
            for name, a in arrays.items()}
    out = nc.dram_tensor("out", (T, D), F32, kind="ExternalOutput").ap()
    decoder_layer(nc, out=out, **args)
    r = run_bass_kernel_spmd(nc, [{name + "_in": a for name, a in arrays.items()}], core_ids=[0])
    return r.results[0]["out"].reshape(B, S, D)
```

```python
from contextlib import ExitStack

import concourse.bass as bass
from concourse import mybir
from concourse.alu_op_type import AluOpType as ALU

ACT = mybir.ActivationFunctionType
F32 = mybir.dt.float32
BF16 = mybir.dt.bfloat16
F32R = mybir.dt.float32r
U32 = mybir.dt.uint32

P = 128
B, S, D = 4, 256, 512
KV = 1601
I = 1376
H, G, HD = 32, 8, 128
E, R = 8, 16
T = B * S
TT = T // P
CT = D // P
NK = B * KV
DROP = I // 2
EPS = 1e-5

GB, GW = 3, 460
IP = GB * GW
IC = (I + P - 1) // P
IR = I - (IC - 1) * P
KT = (NK + P - 1) // P
LAST_KEY = NK - P


def cols(ap, width=P):
    return ap.rearrange("(c p) n -> p c n", p=width)


AHEAD = 32


def done(step):
    return AHEAD + 1 + step


def landed(step):
    return 16 * (AHEAD + 1 + step)


def begin(eng, *sems):
    for x in sems:
        eng.sem_inc(x, AHEAD)


def begin_dma(eng, *sems):
    for x in sems:
        eng.sem_inc(x, 16 * AHEAD)


def wait_apart(eng, sem, value, passed):
    eng.wait_ge(sem, value)
    eng.sem_inc(passed, 1)


class Chain:

    def __init__(self, eng, sem, base=0):
        self.eng, self.sem, self.base, self.n = eng, sem, base, 0

    def done(self, ins):
        self.n += 1
        ins.then_inc(self.sem, 1)

    def wait(self, behind=0):
        self.eng.wait_ge(self.sem, self.base + self.n - behind)

    def wait_apart(self, passed):
        wait_apart(self.eng, self.sem, self.base + self.n, passed)


def product(pe, out, a_hi, a_lo, b_hi, b_lo, start, stop):
    pe.matmul(out, a_hi, b_hi, start=start, stop=False)
    pe.matmul(out, a_hi, b_lo, start=False, stop=False)
    return pe.matmul(out, a_lo, b_hi, start=False, stop=stop)


def gate_and_up(nc, psum, raw, abs_s, xT, WgT, WuT, pS, ahead):
    with ExitStack() as ctx:
        def sb(name, shape, dt=F32):
            return ctx.enter_context(nc.sbuf_tensor(name, shape, dt))

        def sem(name):
            return ctx.enter_context(nc.semaphore(name))

        RAW = 4
        w_raw = raw[:, 0:RAW * I].rearrange("p (r n) -> p r n", r=RAW)
        w_hi = sb("w_hi", [P, 2, CT, IP], F32R)
        w_lo = sb("w_lo", [P, 2, CT, IP], F32R)
        x_raw = sb("x_raw", [P, 2, CT, P])
        x_hi = sb("x_hi", [P, 2, CT, P], F32R)
        x_lo = sb("x_lo", [P, 2, CT, P], F32R)
        s_sb = sb("s_sb", [P, 2, IP])
        p_sb = sb("p_sb", [P, 2, IP])

        w_in = [sem(f"w_in{n}") for n in range(RAW)]
        w_hi_done, w_lo_done, pads = sem("w_hi_done"), sem("w_lo_done"), sem("pads")
        x_in = [sem(f"x_in{s}") for s in range(2)]
        x_hi_done, x_lo_done = sem("x_hi_done"), sem("x_lo_done")
        g_done, u_done = sem("g_done"), sem("u_done")
        s_done, p_done, abs_done = sem("s_done"), sem("p_done"), sem("abs_done")
        p_out = [sem(f"p_out{s}") for s in range(2)]

        g_ps, u_ps = psum[:, 0:GB, 0:GW], psum[:, GB:2 * GB, 0:GW]
        weights = [cols(WgT), cols(WuT)]
        block = ctx.enter_context(nc.Block())

        @block.sync
        def _(sp):
            begin_dma(sp, *x_in, *p_out)

            def load_x(t, s):
                sp.dma_start(x_raw[:, s], cols(xT)[:, :, bass.ds(t * P, P)]).then_inc(x_in[s], 16)

            def store_p(t, s):
                sp.wait_ge(p_done, done(t))
                sp.dma_start(pS[t], p_sb[:, s, 0:I]).then_inc(p_out[s], 16)

            for n in range(2 * CT):
                if n == 1:
                    load_x(0, 0)
                    load_x(1, 1)
                if n >= RAW:
                    sp.wait_ge(w_lo_done, n - RAW + 1)
                sp.dma_start(w_raw[:, n % RAW, :], weights[n // CT][:, n % CT, :]).then_inc(w_in[n % RAW], 16)
            sp.wait_ge(w_lo_done, 2 * CT)
            ahead(sp)
            with sp.Fori(0, TT // 2 - 1) as i:
                for s in range(2):
                    sp.wait_ge(x_lo_done, done(2 * i + s))
                    load_x(2 * i + s + 2, s)
                    store_p(2 * i + s, s)
            for t in (TT - 2, TT - 1):
                store_p(t, t % 2)
            for s in range(2):
                sp.wait_ge(p_out[s], landed(TT // 2 - 1))

        @block.gpsimd
        def _(pool):
            begin(pool, x_lo_done)
            pool.memset(w_hi[:, :, :, I:IP].bitcast(F32), 0.0).then_inc(pads, 1)
            pool.memset(w_lo[:, :, :, I:IP].bitcast(F32), 0.0).then_inc(pads, 1)
            with pool.Fori(0, TT // 2) as i:
                for s in range(2):
                    pool.wait_ge(x_hi_done, done(2 * i + s))
                    pool.tensor_tensor(x_lo[:, s], x_raw[:, s], x_hi[:, s].bitcast(F32), ALU.subtract
                                       ).then_inc(x_lo_done, 1)

        @block.scalar
        def _(act):
            begin(act, x_hi_done, s_done)

            def split_x(t, s, i):
                act.wait_ge(x_in[s], landed(i))
                act.wait_ge(u_done, done(t - 2))
                act.copy(x_hi[:, s], x_raw[:, s]).then_inc(x_hi_done, 1)

            def silu(t, s):
                act.wait_ge(g_done, done(t))
                act.wait_ge(p_done, done(t - 2))
                act.activation(s_sb[:, s].rearrange("p (b n) -> p b n", b=GB), g_ps, ACT.Silu
                               ).then_inc(s_done, 1)

            for n in range(2 * CT):
                act.wait_ge(w_in[n % RAW], 16 * (n // RAW + 1))
                act.copy(w_hi[:, n // CT, n % CT, 0:I], w_raw[:, n % RAW, :]).then_inc(w_hi_done, 1)
                if n == 0:
                    split_x(0, 0, 0)
            silu(0, 0)
            split_x(1, 1, 0)
            silu(1, 1)
            with act.Fori(1, TT // 2) as i:
                for s in range(2):
                    split_x(2 * i + s, s, i)
                    silu(2 * i + s, s)

        @block.vector
        def _(dve):
            begin(dve, p_done, abs_done)
            for n in range(2 * CT):
                dve.wait_ge(w_hi_done, n + 1)
                dve.tensor_tensor(w_lo[:, n // CT, n % CT, 0:I], w_raw[:, n % RAW, :],
                                  w_hi[:, n // CT, n % CT, 0:I].bitcast(F32), ALU.subtract
                                  ).then_inc(w_lo_done, 1)
            with dve.Fori(0, TT // 2) as i:
                for s in range(2):
                    t = 2 * i + s
                    dve.wait_ge(s_done, done(t))
                    dve.tensor_scalar(abs_s[:, t, :].bitcast(U32), s_sb[:, s, 0:I].bitcast(U32),
                                      0x7FFFFFFF, None, ALU.bitwise_and).then_inc(abs_done, 1)
                    dve.wait_ge(u_done, done(t))
                    dve.wait_ge(p_out[s], landed(i - 1))
                    dve.tensor_tensor(p_sb[:, s].rearrange("p (b n) -> p b n", b=GB), u_ps,
                                      s_sb[:, s].rearrange("p (b n) -> p b n", b=GB), ALU.mult
                                      ).then_inc(p_done, 1)

        @block.tensor
        def _(pe):
            begin(pe, g_done, u_done)
            pe.wait_ge(pads, 2)
            with pe.Fori(0, TT // 2) as i:
                for s in range(2):
                    t = 2 * i + s
                    pe.wait_ge(x_lo_done, done(t))
                    for m, free, ready in ((0, s_done, g_done), (1, p_done, u_done)):
                        pe.wait_ge(free, done(t - 1))
                        for c in range(CT):
                            pe.wait_ge(w_lo_done, CT * m + c + 1)
                            for b in range(GB):
                                w = slice(b * GW, (b + 1) * GW)
                                last = product(pe, psum[:, GB * m + b, 0:GW], x_hi[:, s, c], x_lo[:, s, c],
                                               w_hi[:, m, c, w], w_lo[:, m, c, w], c == 0, c == CT - 1)
                        last.then_inc(ready, 1)


class KeyValueWeights:
    N = G * HD
    CHUNKS = 2 * N // 512 * CT
    SLOTS = IC

    def __init__(self, nc, ctx, raw, WkT, WvT):
        self.raw = raw.rearrange("p (r n) -> p r n", r=self.SLOTS)
        self.weights = WkT, WvT
        self.landed = [ctx.enter_context(nc.semaphore(f"kvw_in{s}")) for s in range(self.SLOTS)]

    def load(self, sp, n):
        half = self.CHUNKS // 2
        j = n % half // CT
        sp.dma_start(self.raw[:, n % self.SLOTS], cols(self.weights[n // half])[:, n % CT, j * 512:(j + 1) * 512]
                     ).then_inc(self.landed[n % self.SLOTS], 16)

    def first_loads(self, sp):
        for n in range(self.SLOTS):
            self.load(sp, n)

    def wait(self, eng, n):
        eng.wait_ge(self.landed[n % self.SLOTS], 16 * (n // self.SLOTS + 1))


def keys_and_values(nc, psum, ident, abs_s, thr, n_less, weights, ctxT, kS, vS, ahead):
    with ExitStack() as ctx:
        def sb(name, shape, dt=F32):
            return ctx.enter_context(nc.sbuf_tensor(name, shape, dt))

        def sem(name):
            return ctx.enter_context(nc.semaphore(name))

        N = G * HD
        NB = N // 512
        RING = 3
        STEPS = KT // RING - 1
        BITS = 2
        assert KT == RING * (STEPS + 1) and BITS * STEPS >= 31
        w_raw, SLOTS = weights.raw, weights.SLOTS
        w_hi = sb("kvw_hi", [P, 2 * NB, CT, 512], F32R)
        w_lo = sb("kvw_lo", [P, 2 * NB, CT, 512], F32R)
        c_raw = sb("c_raw", [P, RING, CT, P])
        c_hi = sb("c_hi", [P, RING, CT, P], F32R)
        c_lo = sb("c_lo", [P, RING, CT, P], F32R)
        square = sb("square", [P, N])
        ssq = sb("ssq", [P, RING, G])
        var = sb("var", [P, RING, G])
        rstd = sb("rstd", [P, RING, G])
        minus_half = sb("minus_half", [P, G])
        k_sb = sb("k_sb", [P, N])
        v_sb = sb("v_sb", [P, 2, N])
        kT_sb = sb("kT_sb", [P, 2, N])
        bit = sb("bit", [P, TT], U32)
        cand = sb("cand", [P, TT], U32)
        less = sb("less", [P, TT])
        below = sb("below", [P, TT], U32)
        flags = sb("flags", [P, 2, I], BF16)

        w_hi_done, w_lo_done, half = sem("kvw_hi_done"), sem("kvw_lo_done"), sem("half")
        c_in = [sem(f"c_in{s}") for s in range(RING)]
        c_hi_done, c_lo_done = sem("c_hi_done"), sem("c_lo_done")
        k_done, v_done, kT_done = sem("k_done"), sem("v_done"), sem("kT_done")
        ssq_done, var_done, rstd_done = sem("ssq_done"), sem("var_done"), sem("rstd_done")
        k_sb_done, v_sb_done, kT_sb_done = sem("k_sb_done"), sem("v_sb_done"), sem("kT_sb_done")
        v_out = [sem(f"v_out{s}") for s in range(2)]
        kT_out = [sem(f"kT_out{s}") for s in range(2)]
        chain = sem("bit_chain")
        pool_passed, dve_passed, sp_passed = sem("pool_passed_k"), sem("dve_passed_k"), sem("sp_passed_k")

        def k_banks(s):
            return psum[:, NB * s:NB * s + NB, :].rearrange("p b n -> p (b n)")

        v_bank = NB * RING
        v_ps = psum[:, v_bank:v_bank + NB, :].rearrange("p b n -> p (b n)")
        block = ctx.enter_context(nc.Block())

        BODY = 2 * RING
        TRIPS = STEPS // 2

        def tiles(eng, step, trips=TRIPS):
            with eng.Fori(0, trips) as i:
                for s in range(BODY):
                    step(i, s)
            for t in range(BODY * trips, KT):
                step(t // BODY, t % BODY)

        def fresh(i, s):
            t = BODY * i + s
            return (LAST_KEY, KT * P - NK) if isinstance(i, int) and t == KT - 1 else (t * P, 0)

        def is_tile(i, s):
            return not isinstance(i, int) or BODY * i + s < KT

        @block.sync
        def _(sp):
            begin_dma(sp, *c_in, *v_out, *kT_out)

            def load_c(i, s):
                sp.wait_ge(c_lo_done, done(BODY * i + s - RING))
                sp.dma_start(c_raw[:, s % RING], cols(ctxT)[:, :, bass.ds(fresh(i, s)[0], P)]
                             ).then_inc(c_in[s % RING], 16)

            def store(i, s):
                t, r = BODY * i + s, s % 2
                start, old = fresh(i, s)
                at = bass.ds(start + old, P - old)
                sp.wait_ge(v_sb_done, done(t))
                sp.dma_start(vS[at, :], v_sb[old:P, r]).then_inc(v_out[r], 16)
                wait_apart(sp, kT_sb_done, done(t), sp_passed)
                sp.dma_start(kS[:, :, at].rearrange("g d k -> d g k"),
                             kT_sb[:, r].rearrange("d (g k) -> d g k", g=G)[:, :, old:P]).then_inc(kT_out[r], 16)

            for t in range(RING):
                load_c(0, t)
            for n in range(SLOTS, weights.CHUNKS):
                sp.wait_ge(w_lo_done, n - SLOTS + 1)
                weights.load(sp, n)

            def step(i, s):
                if is_tile(i, s + RING):
                    load_c(i, s + RING)
                store(i, s)

            sp.wait_ge(w_lo_done, weights.CHUNKS)
            ahead(sp)
            tiles(sp, step, TRIPS - 1)
            for s in range(2):
                sp.wait_ge(v_out[s], landed((KT - 1 - s) // 2))
                sp.wait_ge(kT_out[s], landed((KT - 1 - s) // 2))

        @block.gpsimd
        def _(pool):
            begin(pool, c_lo_done, var_done, rstd_done)
            pool.memset(minus_half[:], -0.5).then_inc(half, 1)
            pool.wait_ge(half, 1)

            def split_c(i, s):
                pool.wait_ge(c_hi_done, done(BODY * i + s))
                pool.tensor_tensor(c_lo[:, s % RING], c_raw[:, s % RING], c_hi[:, s % RING].bitcast(F32),
                                   ALU.subtract).then_inc(c_lo_done, 1)

            def step(i, s):
                t, r = BODY * i + s, s % RING
                wait_apart(pool, ssq_done, done(t), pool_passed)
                pool.tensor_scalar(var[:, r], ssq[:, r], 1.0 / HD, EPS, ALU.mult, ALU.add).then_inc(var_done, 1)
                pool.wait_ge(var_done, done(t))
                pool.tensor_tensor(rstd[:, r], var[:, r], minus_half[:], ALU.pow).then_inc(rstd_done, 1)
                if is_tile(i, s + 2):
                    split_c(i, s + 2)

            split_c(0, 0)
            split_c(0, 1)
            tiles(pool, step)

        @block.scalar
        def _(act):
            begin(act, c_hi_done, ssq_done, v_sb_done, kT_sb_done)

            def split_c(i, s):
                act.wait_ge(c_in[s % RING], landed(2 * i + s // RING))
                act.wait_ge(v_done, done(BODY * i + s - RING))
                act.copy(c_hi[:, s % RING], c_raw[:, s % RING]).then_inc(c_hi_done, 1)

            split_c(0, 0)
            split_c(0, 1)
            for n in range(2 * NB * CT):
                weights.wait(act, n)
                act.copy(w_hi[:, n // CT, n % CT], w_raw[:, n % SLOTS]).then_inc(w_hi_done, 1)

            def step(i, s):
                t, use2 = BODY * i + s, BODY // 2 * i + s // 2
                act.wait_ge(k_done, done(t))
                act.wait_ge(ssq_done, done(t - 1))
                for g in range(G):
                    last = act.activation(square[:, g * HD:(g + 1) * HD], k_banks(s % RING)[:, g * HD:(g + 1) * HD], ACT.Square,
                                          accum_out=ssq[:, s % RING, g:g + 1])
                last.then_inc(ssq_done, 1)
                act.wait_ge(v_done, done(t))
                act.wait_ge(v_out[s % 2], landed(use2 - 1))
                act.copy(v_sb[:, s % 2], v_ps).then_inc(v_sb_done, 1)
                if is_tile(i, s + 2):
                    split_c(i, s + 2)
                act.wait_ge(kT_done, done(t))
                act.wait_ge(kT_out[s % 2], landed(use2 - 1))
                act.copy(kT_sb[:, s % 2], k_banks(s % RING)).then_inc(kT_sb_done, 1)

            tiles(act, step)

        @block.vector
        def _(dve):
            begin(dve, k_sb_done)
            for n in range(2 * NB * CT):
                dve.wait_ge(w_hi_done, n + 1)
                dve.tensor_tensor(w_lo[:, n // CT, n % CT], w_raw[:, n % SLOTS], w_hi[:, n // CT, n % CT].bitcast(F32),
                                  ALU.subtract).then_inc(w_lo_done, 1)
            bits = Chain(dve, chain)
            bits.done(dve.memset(thr[:].bitcast(F32), 0.0))
            bits.done(dve.memset(bit[:].bitcast(F32), 2.0))

            def count(at, tt, out):
                bits.wait(behind=1)
                bits.done(dve.tensor_scalar(flags[:, tt % 2], abs_s[:, tt], at[:, tt:tt + 1].bitcast(F32), 0.0,
                                            ALU.is_lt, ALU.add, accum_out=out[:, tt:tt + 1]))

            def norm_keys(i, s):
                t = BODY * i + s
                dve.wait_ge(rstd_done, done(t))
                dve.wait_ge(kT_done, done(t - 1))
                dve.tensor_tensor(k_sb[:].rearrange("p (g d) -> p g d", g=G),
                                  k_banks(s % RING).rearrange("p (g d) -> p g d", g=G),
                                  rstd[:, s % RING].unsqueeze(2).to_broadcast((P, G, HD)), ALU.mult
                                  ).then_inc(k_sb_done, 1)

            first = bits.n
            with dve.Fori(0, TRIPS) as i:
                per_trip = BITS * 2 * (TT + 4)
                bits.base, bits.n = first + per_trip * i, 0
                for s in range(BODY):
                    norm_keys(i, s)
                    for q in range(BITS * 2 * TT * s // BODY, BITS * 2 * TT * (s + 1) // BODY):
                        if q % TT == 0:
                            bits.wait()
                            bits.done(dve.tensor_tensor(cand[:], thr[:], bit[:], ALU.bitwise_or))
                            bits.wait()
                        count(cand, q % TT, less)
                        if q % TT == TT - 1:
                            bits.done(dve.tensor_scalar(bit[:], bit[:], 1, None, ALU.logical_shift_right))
                            bits.wait()
                            bits.done(dve.tensor_scalar(below[:], less[:], DROP - 0.5, None, ALU.is_lt))
                            bits.wait_apart(dve_passed)
                            bits.done(dve.copy_predicated(thr[:], below[:], cand[:]))
                assert bits.n == per_trip
            bits.base, bits.n = first, per_trip * TRIPS
            bits.wait()
            for s in range(KT - BODY * TRIPS):
                norm_keys(TRIPS, s)
                for tt in range(TT * s // 3, TT * (s + 1) // 3):
                    count(thr, tt, n_less)
            bits.wait()

        @block.tensor
        def _(pe):
            begin(pe, k_done, v_done, kT_done)

            def project(i, s, which, out, first=False):
                for j in range(NB):
                    for c in range(CT):
                        m = NB * which + j
                        if first:
                            pe.wait_ge(w_lo_done, CT * m + c + 1)
                        last = product(pe, out[:, j * 512:(j + 1) * 512], c_hi[:, s % RING, c], c_lo[:, s % RING, c],
                                       w_hi[:, m, c], w_lo[:, m, c], c == 0, c == CT - 1)
                return last

            def keys(i, s, first=False):
                pe.wait_ge(c_lo_done, done(BODY * i + s))
                pe.wait_ge(kT_sb_done, done(BODY * i + s - RING))
                project(i, s, 0, k_banks(s % RING), first).then_inc(k_done, 1)

            def values(i, s, first=False):
                pe.wait_ge(v_sb_done, done(BODY * i + s - 1))
                project(i, s, 1, v_ps, first).then_inc(v_done, 1)

            def transpose(i, s):
                pe.wait_ge(k_sb_done, done(BODY * i + s))
                for g in range(G):
                    last = pe.transpose(k_banks(s % RING)[:, g * P:(g + 1) * P], k_sb[:, g * HD:(g + 1) * HD], ident)
                last.then_inc(kT_done, 1)

            def step(i, s):
                if is_tile(i, s + 1):
                    keys(i, s + 1)
                transpose(i, s)
                if is_tile(i, s + 1):
                    values(i, s + 1)

            keys(0, 0, True)
            values(0, 0, True)
            tiles(pe, step)


def make_identity(nc, ident):
    with nc.semaphore("ident_done") as ident_done, nc.Block() as block:
        @block.gpsimd
        def _(pool):
            pool.memset(ident, 0.0).then_inc(ident_done, 1)
            pool.wait_ge(ident_done, 1)
            pool.affine_select(out=ident, in_=ident, compare_op=ALU.not_equal, fill=1.0, base=0,
                               pattern=[[-1, P]], channel_multiplier=1).then_inc(ident_done, 1)
            pool.wait_ge(ident_done, 2)


class DownInputs:

    def __init__(self, nc, ctx, raw, x, WdT, pS):
        self.x, self.WdT, self.pS = x, WdT, pS
        self.w_raw = raw.rearrange("p (c n) -> p c n", c=IC)
        self.p_sb = ctx.enter_context(nc.sbuf_tensor("pd_sb", [P, 2, IC * P], F32))
        self.x_sb = ctx.enter_context(nc.sbuf_tensor("xd_sb", [P, 2, D], F32))
        self.w_in = ctx.enter_context(nc.semaphore("wd_in"))
        self.p_in = [ctx.enter_context(nc.semaphore(f"pd_in{s}")) for s in range(2)]
        self.x_in = [ctx.enter_context(nc.semaphore(f"xd_in{s}")) for s in range(2)]

    def load_p(self, sp, t, s):
        sp.dma_start(self.p_sb[:, s, 0:I], self.pS[t]).then_inc(self.p_in[s], 16)

    def load_x(self, sp, t, s):
        sp.dma_start(self.x_sb[:, s], self.x[bass.ds(t * P, P), :]).then_inc(self.x_in[s], 16)

    def first_loads(self, sp):
        begin_dma(sp, *self.p_in, *self.x_in)
        full = (IC - 1) * P
        sp.dma_start(self.w_raw[:, 0:IC - 1], cols(self.WdT[0:full, :])).then_inc(self.w_in, 16)
        sp.dma_start(self.w_raw[0:IR, IC - 1], self.WdT[full:I, :]).then_inc(self.w_in, 16)
        for s in range(2):
            self.load_p(sp, s, s)
            self.load_x(sp, s, s)


def down_and_norm(nc, psum, ident, abs_s, thr, n_less, x1T_hi, x1T_lo, inputs, x1S, ahead):
    with ExitStack() as ctx:
        def sb(name, shape, dt=F32):
            return ctx.enter_context(nc.sbuf_tensor(name, shape, dt))

        def sem(name):
            return ctx.enter_context(nc.semaphore(name))

        w_raw, p_sb, x_sb = inputs.w_raw, inputs.p_sb, inputs.x_sb
        w_hi = sb("wd_hi", [P, IC, D], F32R)
        w_lo = sb("wd_lo", [P, IC, D], F32R)
        need = sb("need", [P, TT])
        keep = sb("keep", [P, 2, I])
        order = sb("order", [P, I])
        hT_hi = sb("hT_hi", [P, 2, IC * P], F32R)
        hT_lo = sb("hT_lo", [P, 2, IC * P], F32R)
        y_sb = sb("yd_sb", [P, 2, D])
        stats = sb("stats_d", [P, 2, 6])
        mv = sb("mv_d", [P, 2, 2])
        rstd = sb("rstd_d", [P, 2])
        minus_half = sb("minus_half_d", [P, 1])
        x1_sb = sb("x1_sb", [P, 2, D])

        w_in, p_in, x_in = inputs.w_in, inputs.p_in, inputs.x_in
        w_hi_done, pads, w_pads = sem("wd_hi_done"), sem("pads_d"), sem("w_pads")
        w_lo_pool, w_lo_dve = sem("wd_lo_pool"), sem("wd_lo_dve")
        chain = sem("chain_d")
        keep_done, h_done, hT_done = sem("keep_done"), sem("h_done"), sem("hT_done")
        hT_hi_done, hT_lo_done = sem("hT_hi_done"), sem("hT_lo_done")
        down_done, mv_done, rstd_done = sem("down_done"), sem("mv_done"), sem("rstd_done_d")
        x1_done, x1T_done, x1T_hi_done, x1T_lo_done = (sem("x1_done"), sem("x1T_done"), sem("x1T_hi_done"),
                                                       sem("x1T_lo_done"))
        x1_out = [sem(f"x1_out{s}") for s in range(2)]
        dve_passed = sem("dve_passed_d")

        POOL_W = 8

        def hT_ps(s):
            return psum[:, 3 * s:3 * s + 3, :].rearrange("p b n -> p (b n)")[:, 0:IC * P]

        def y_ps(s):
            return psum[:, 6 + s, :]

        FIRST, LAST = 1, TT - 4

        def steps(eng, step):
            step(0, 0)
            with eng.Fori(0, (LAST - FIRST + 1) // 2) as i:
                for m in range(FIRST, FIRST + 2):
                    step(i, m)
            for m in range(LAST + 1, TT):
                step(0, m)

        def is_tile(i, m):
            return not isinstance(i, int) or 0 <= 2 * i + m < TT

        block = ctx.enter_context(nc.Block())

        @block.sync
        def _(sp):
            begin_dma(sp, *x1_out)

            def store(i, m):
                sp.wait_ge(x1_done, done(2 * i + m))
                sp.dma_start(x1S[bass.ds((2 * i + m) * P, P), :], x1_sb[:, m % 2]).then_inc(x1_out[m % 2], 16)

            def step(i, m):
                if isinstance(i, int) and m == LAST + 1:
                    sp.wait_ge(w_lo_pool, POOL_W)
                    sp.wait_ge(w_lo_dve, IC - POOL_W)
                    ahead(sp)
                if is_tile(i, m + 2):
                    sp.wait_ge(hT_done, done(2 * i + m))
                    inputs.load_p(sp, 2 * i + m + 2, m % 2)
                if is_tile(i, m - 1):
                    store(i, m - 1)
                    if is_tile(i, m + 1):
                        inputs.load_x(sp, 2 * i + m + 1, (m + 1) % 2)

            steps(sp, step)
            store(0, TT - 1)
            for s in range(2):
                sp.wait_ge(x1_out[s], landed(TT // 2 - 1))

        @block.gpsimd
        def _(pool):
            begin(pool, h_done, rstd_done)
            pool.memset(minus_half[:], -0.5).then_inc(pads, 1)
            pool.memset(p_sb[:, :, I:IC * P], 0.0).then_inc(pads, 1)
            pool.wait_ge(pads, 2)

            def gates(i, m):
                pool.wait_ge(keep_done, done(2 * i + m))
                pool.wait_ge(p_in[m % 2], landed(i + m // 2))
                pool.tensor_tensor(p_sb[:, m % 2, 0:I], p_sb[:, m % 2, 0:I], keep[:, m % 2], ALU.mult
                                   ).then_inc(h_done, 1)

            def root(i, m):
                s = m % 2
                pool.wait_ge(mv_done, done(2 * i + m))
                pool.tensor_tensor(rstd[:, s:s + 1], mv[:, s, 1:2], minus_half[:], ALU.pow).then_inc(rstd_done, 1)

            def split_w(n):
                rows = P if n < IC - 1 else IR
                pool.wait_ge(w_hi_done, n + 1)
                pool.tensor_tensor(w_lo[0:rows, n], w_raw[0:rows, n], w_hi[0:rows, n].bitcast(F32), ALU.subtract
                                   ).then_inc(w_lo_pool, 1)

            for s in range(2):
                for n in range(POOL_W // 2 * s, POOL_W // 2 * (s + 1)):
                    split_w(n)
                gates(0, s)
            gates(0, 2)

            def step(i, m):
                if is_tile(i, m - 1):
                    root(i, m - 1)
                if is_tile(i, m + 3):
                    gates(i, m + 3)

            steps(pool, step)
            root(0, TT - 1)

        @block.scalar
        def _(act):
            begin(act, hT_hi_done, x1T_hi_done)
            act.wait_ge(w_in, 32)
            for n in range(IC):
                rows = P if n < IC - 1 else IR
                act.copy(w_hi[0:rows, n], w_raw[0:rows, n]).then_inc(w_hi_done, 1)

            def gates(i, m):
                act.wait_ge(hT_done, done(2 * i + m))
                act.wait_ge(down_done, done(2 * i + m - 2))
                act.copy(hT_hi[:, m % 2], hT_ps(m % 2)).then_inc(hT_hi_done, 1)

            def x1(i, m):
                act.wait_ge(x1T_done, done(2 * i + m))
                act.copy(x1T_hi[:, :, bass.ds((2 * i + m) * P, P)], y_ps(m % 2).rearrange("p (c n) -> p c n", c=CT)
                         ).then_inc(x1T_hi_done, 1)

            def step(i, m):
                if is_tile(i, m + 1):
                    gates(i, m + 1)
                if is_tile(i, m - 1):
                    x1(i, m - 1)

            gates(0, 0)
            steps(act, step)
            x1(0, TT - 1)

        @block.vector
        def _(dve):
            begin(dve, keep_done, hT_lo_done, mv_done, x1_done, x1T_lo_done)
            dve.memset(w_hi[IR:P, IC - 1, :].bitcast(F32), 0.0).then_inc(w_pads, 1)
            dve.memset(w_lo[IR:P, IC - 1, :].bitcast(F32), 0.0).then_inc(w_pads, 1)
            own = Chain(dve, chain)
            own.done(dve.tensor_scalar(need[:], n_less[:], -1.0, float(DROP), ALU.mult, ALU.add))

            def choose(i, m):
                t, s = 2 * i + m, m % 2
                at = thr[:, bass.ds(t, 1)].bitcast(F32)
                own.wait()
                dve.wait_ge(h_done, done(t - 2))
                own.done(dve.tensor_scalar(keep[:, s], abs_s[:, t], at, None, ALU.is_equal))
                own.wait()
                own.done(dve.tensor_tensor_scan(order[:], keep[:, s], keep[:, s], 0.0, ALU.add, ALU.max))
                own.wait()
                own.done(dve.scalar_tensor_tensor(order[:], order[:], need[:, bass.ds(t, 1)], keep[:, s],
                                                  ALU.is_gt, ALU.mult))
                own.wait()
                dve.scalar_tensor_tensor(keep[:, s], abs_s[:, t], at, order[:], ALU.is_gt, ALU.add
                                         ).then_inc(keep_done, 1)
                dve.wait_ge(keep_done, done(t))

            def split_gates(i, m):
                s = m % 2
                dve.wait_ge(hT_hi_done, done(2 * i + m))
                dve.tensor_tensor(hT_lo[:, s], hT_ps(s), hT_hi[:, s].bitcast(F32), ALU.subtract
                                  ).then_inc(hT_lo_done, 1)

            def norm(i, m):
                t, s = 2 * i + m, m % 2
                dve.wait_ge(down_done, done(t))
                dve.wait_ge(x_in[s], landed(i + m // 2))
                own.done(dve.tensor_tensor(y_sb[:, s], y_ps(s), x_sb[:, s], ALU.add))
                own.wait()
                own.done(dve.bn_stats(stats[:, s], y_sb[:, s]))
                own.wait_apart(dve_passed)
                own.done(dve.bn_aggr(mv[:, s], stats[:, s]))
                own.wait()
                dve.tensor_scalar(mv[:, s, 1:2], mv[:, s, 1:2], EPS, None, ALU.add).then_inc(mv_done, 1)
                dve.wait_ge(rstd_done, done(t))
                dve.wait_ge(x1_out[s], landed(i + m // 2 - 1))
                dve.wait_ge(x1T_done, done(t - 2))
                dve.tensor_scalar(x1_sb[:, s], y_sb[:, s], mv[:, s, 0:1], rstd[:, s:s + 1], ALU.subtract,
                                  ALU.mult).then_inc(x1_done, 1)

            def split_x1(i, m):
                t, s = 2 * i + m, m % 2
                dve.wait_ge(x1T_hi_done, done(t))
                at = bass.ds(t * P, P)
                dve.tensor_tensor(x1T_lo[:, :, at], y_ps(s).rearrange("p (c n) -> p c n", c=CT),
                                  x1T_hi[:, :, at].bitcast(F32), ALU.subtract).then_inc(x1T_lo_done, 1)

            choose(0, 0)
            for n in range(POOL_W, IC):
                rows = P if n < IC - 1 else IR
                dve.wait_ge(w_hi_done, n + 1)
                dve.tensor_tensor(w_lo[0:rows, n], w_raw[0:rows, n], w_hi[0:rows, n].bitcast(F32),
                                  ALU.subtract).then_inc(w_lo_dve, 1)
            choose(0, 1)
            split_gates(0, 0)
            choose(0, 2)

            def step(i, m):
                if is_tile(i, m - 1):
                    norm(i, m - 1)
                if is_tile(i, m + 1):
                    split_gates(i, m + 1)
                if is_tile(i, m - 1):
                    split_x1(i, m - 1)
                if is_tile(i, m + 3):
                    choose(i, m + 3)

            step(0, 0)
            before, per_trip, trips = own.n, 12, (LAST - FIRST + 1) // 2
            with dve.Fori(0, trips) as i:
                own.base, own.n = before + per_trip * i, 0
                for m in range(FIRST, FIRST + 2):
                    step(i, m)
                assert own.n == per_trip
            own.base, own.n = before, per_trip * trips
            for m in range(LAST + 1, TT):
                step(0, m)
            norm(0, TT - 1)
            split_x1(0, TT - 1)

        @block.tensor
        def _(pe):
            begin(pe, hT_done, down_done, x1T_done)
            pe.wait_ge(pads, 2)
            pe.wait_ge(w_pads, 2)

            def transpose_gates(i, m):
                pe.wait_ge(h_done, done(2 * i + m))
                pe.wait_ge(hT_lo_done, done(2 * i + m - 2))
                for c in range(IC):
                    last = pe.transpose(hT_ps(m % 2)[:, c * P:(c + 1) * P], p_sb[:, m % 2, c * P:(c + 1) * P], ident)
                last.then_inc(hT_done, 1)

            def down(i, m, tiles):
                for c in tiles:
                    if c == 0:
                        pe.wait_ge(hT_lo_done, done(2 * i + m))
                        pe.wait_ge(x1T_lo_done, done(2 * i + m - 2))
                    if isinstance(i, int) and m == 0:
                        pe.wait_ge(*((w_lo_pool, c + 1) if c < POOL_W else (w_lo_dve, c + 1 - POOL_W)))
                    k = slice(c * P, (c + 1) * P)
                    last = product(pe, y_ps(m % 2), hT_hi[:, m % 2, k], hT_lo[:, m % 2, k], w_hi[:, c], w_lo[:, c],
                                   c == 0, c == IC - 1)
                    if c == IC - 1:
                        last.then_inc(down_done, 1)

            def transpose_x1(i, m):
                pe.wait_ge(x1_done, done(2 * i + m))
                for c in range(CT):
                    last = pe.transpose(y_ps(m % 2)[:, c * P:(c + 1) * P], x1_sb[:, m % 2, c * P:(c + 1) * P], ident)
                last.then_inc(x1T_done, 1)

            def step(i, m):
                down(i, m, range(IC // 2))
                if is_tile(i, m - 1):
                    transpose_x1(i, m - 1)
                down(i, m, range(IC // 2, IC))
                if is_tile(i, m + 2):
                    transpose_gates(i, m + 2)

            transpose_gates(0, 0)
            transpose_gates(0, 1)
            steps(pe, step)
            transpose_x1(0, TT - 1)


class QueryWeights:
    W = H // G * HD

    def __init__(self, nc, ctx, raw, WqT):
        self.raw = raw[:, 0:2 * CT * self.W].rearrange("p (r c n) -> p r c n", r=2, c=CT)
        self.WqT = WqT
        self.landed = [ctx.enter_context(nc.semaphore(f"wq_in{s}")) for s in range(2)]

    def load(self, sp, group, r):
        sp.dma_start(self.raw[:, r], cols(self.WqT)[:, :, bass.ds(group * self.W, self.W)]).then_inc(self.landed[r], 16)

    def first_loads(self, sp):
        begin_dma(sp, *self.landed)
        self.load(sp, 0, 0)
        self.load(sp, 1, 1)


def queries(nc, psum, ident, x1T_hi, x1T_lo, weights, qn, kn, qS, ahead):
    with ExitStack() as ctx:
        def sb(name, shape, dt=F32):
            return ctx.enter_context(nc.sbuf_tensor(name, shape, dt))

        def sem(name):
            return ctx.enter_context(nc.semaphore(name))

        HG = H // G
        W = HG * HD
        BODY = 2 * TT
        TRIPS = G // 2
        LAG = 3
        w_raw = weights.raw
        w_hi = sb("wq_hi", [P, 2, CT, W], F32R)
        w_lo = sb("wq_lo", [P, 2, CT, W], F32R)
        wn = sb("wn", [P, 2])
        w_qk = sb("w_qk", [P, 1])
        minus_half = sb("minus_half_q", [P, HG])
        square = sb("square_q", [P, 2, W])
        ssq = sb("ssq_q", [P, TT, HG])
        var = sb("var_q", [P, TT, HG])
        rstd = sb("rstd_q", [P, TT, HG])
        q_sb = sb("q_sb", [P, 4, W])
        qT_sb = sb("qT_sb", [P, 4, W])

        w_in = weights.landed
        wn_in, half = sem("wn_in"), sem("half_q")
        w_hi_done, w_lo_done, w_qk_done = sem("wq_hi_done"), sem("wq_lo_done"), sem("w_qk_done")
        q_done, ssq_done, var_done, rstd_done = sem("q_done"), sem("ssq_q"), sem("var_done_q"), sem("rstd_done_q")
        q_sb_done, qT_done, qT_sb_done = sem("q_sb_done"), sem("qT_done"), sem("qT_sb_done")
        qT_out = [sem(f"qT_out{s}") for s in range(4)]

        def steps(eng, step, ahead=0):
            with eng.Fori(0, TRIPS - 1) as i:
                for s in range(BODY):
                    step(i, s)
            for s in range(BODY):
                step(TRIPS - 1, s)

        def last_trip(i):
            return isinstance(i, int) and i == TRIPS - 1

        block = ctx.enter_context(nc.Block())

        @block.sync
        def _(sp):
            begin_dma(sp, *qT_out)
            sp.dma_start(wn[:, 0:1], qn).then_inc(wn_in, 16)
            sp.dma_start(wn[:, 1:2], kn).then_inc(wn_in, 16)

            def load_w(i, r):
                sp.wait_ge(w_lo_done, done(CT * (2 * i + r - 1) - 1))
                weights.load(sp, 2 * i + r, r)

            def step(i, s):
                if s % TT == 0 and not last_trip(i):
                    load_w(i + 1, s // TT)
                if s == TT and last_trip(i):
                    sp.wait_ge(w_lo_done, done(CT * G - 1))
                    for r in range(4):
                        sp.wait_ge(qT_out[r], landed(BODY // 4))
                    ahead(sp)
                sp.wait_ge(qT_sb_done, done(BODY * i + s))
                t, b = s % TT, s % TT // (S // P)
                at = slice((t - b * (S // P)) * P, (t - b * (S // P) + 1) * P)
                sp.dma_start(qS[b, 2 * i + s // TT, :, :, at], qT_sb[:, s % 4].rearrange("d (h q) -> d h q", h=HG)
                             ).then_inc(qT_out[s % 4], 16)

            steps(sp, step)
            for s in range(4):
                sp.wait_ge(qT_out[s], landed(BODY * TRIPS // 4 - 1))

        @block.gpsimd
        def _(pool):
            begin(pool, rstd_done)
            pool.memset(minus_half[:], -0.5).then_inc(half, 1)
            pool.wait_ge(half, 1)

            def step(i, s):
                pool.wait_ge(var_done, done(BODY * i + s))
                pool.tensor_tensor(rstd[:, s % TT], var[:, s % TT], minus_half[:], ALU.pow).then_inc(rstd_done, 1)

            steps(pool, step)

        @block.scalar
        def _(act):
            begin(act, w_hi_done, ssq_done, qT_sb_done)
            act.wait_ge(w_qk_done, 1)

            def split_w(i, r, c):
                act.wait_ge(w_in[r], landed(i))
                act.wait_ge(q_done, done(BODY * i + TT * (r + 1) - 1 - BODY))
                act.copy(w_hi[:, r, c], w_raw[:, r, c]).then_inc(w_hi_done, 1)

            def squares(i, s):
                n = BODY * i + s
                act.wait_ge(q_done, done(n))
                act.wait_ge(ssq_done, done(n - 2))
                for h in range(HG):
                    last = act.activation(square[:, s % 2, h * HD:(h + 1) * HD], psum[:, s % TT, h * HD:(h + 1) * HD],
                                          ACT.Square, accum_out=ssq[:, s % TT, h:h + 1])
                last.then_inc(ssq_done, 1)

            def step(i, s):
                n = BODY * i + s
                if not (last_trip(i) and s + LAG >= BODY):
                    squares(i, s + LAG)
                act.wait_ge(qT_done, done(n))
                act.wait_ge(qT_out[s % 4], landed(BODY // 4 * i + s // 4 - 1))
                act.mul(qT_sb[:, s % 4], psum[:, s % TT], w_qk[:, 0:1]).then_inc(qT_sb_done, 1)
                if s % TT < CT and not (last_trip(i) and s >= TT):
                    split_w(i + s // TT, 1 - s // TT, s % TT)

            for c in range(CT):
                split_w(0, 0, c)
            for s in range(LAG):
                squares(0, s)
            steps(act, step)

        @block.vector
        def _(dve):
            begin(dve, w_lo_done, var_done, q_sb_done)
            dve.wait_ge(wn_in, 32)
            dve.scalar_tensor_tensor(w_qk[:], wn[:, 0:1], -float(HD) ** -0.5, wn[:, 1:2], ALU.mult, ALU.mult
                                     ).then_inc(w_qk_done, 1)

            def split_w(i, r, c):
                dve.wait_ge(w_hi_done, done(CT * (2 * i + r) + c))
                dve.tensor_tensor(w_lo[:, r, c], w_raw[:, r, c], w_hi[:, r, c].bitcast(F32), ALU.subtract
                                  ).then_inc(w_lo_done, 1)

            def variance(i, s):
                dve.wait_ge(ssq_done, done(BODY * i + s))
                dve.tensor_scalar(var[:, s % TT], ssq[:, s % TT], 1.0 / HD, EPS, ALU.mult, ALU.add
                                  ).then_inc(var_done, 1)

            def norm(i, s):
                n = BODY * i + s
                dve.wait_ge(rstd_done, done(n))
                dve.wait_ge(qT_done, done(n - 4))
                dve.tensor_tensor(q_sb[:, s % 4].rearrange("p (h d) -> p h d", h=HG),
                                  psum[:, s % TT].rearrange("p (h d) -> p h d", h=HG),
                                  rstd[:, s % TT].unsqueeze(2).to_broadcast((P, HG, HD)), ALU.mult
                                  ).then_inc(q_sb_done, 1)

            def step(i, s):
                if not (last_trip(i) and s + 2 >= BODY):
                    variance(i, s + 2)
                norm(i, s)
                if s % TT < CT and not (last_trip(i) and s >= TT):
                    split_w(i + s // TT, 1 - s // TT, s % TT)

            for c in range(CT):
                split_w(0, 0, c)
            variance(0, 0)
            variance(0, 1)
            steps(dve, step)

        @block.tensor
        def _(pe):
            begin(pe, q_done, qT_done)

            def project(i, s):
                i, s = (i + 1, s - BODY) if s >= BODY else (i, s)
                r, t = s // TT, s % TT
                pe.wait_ge(qT_sb_done, done(BODY * i + s - TT))
                for c in range(CT):
                    if t == 0:
                        pe.wait_ge(w_lo_done, done(CT * (2 * i + r) + c))
                    at = slice(t * P, (t + 1) * P)
                    last = product(pe, psum[:, t], x1T_hi[:, c, at], x1T_lo[:, c, at], w_hi[:, r, c], w_lo[:, r, c],
                                   c == 0, c == CT - 1)
                last.then_inc(q_done, 1)

            def step(i, s):
                if not (last_trip(i) and s + LAG >= BODY):
                    project(i, s + LAG)
                pe.wait_ge(q_sb_done, done(BODY * i + s))
                for h in range(HG):
                    last = pe.transpose(psum[:, s % TT, h * P:(h + 1) * P], q_sb[:, s % 4, h * HD:(h + 1) * HD], ident)
                last.then_inc(qT_done, 1)

            for s in range(LAG):
                project(0, s)
            steps(pe, step)


class AttentionInputs:
    SB, SW = 4, 402
    KP = SB * SW
    NT = (KV + P - 1) // P
    KR = KV - (NT - 1) * P
    QW = 2 * S

    def __init__(self, nc, ctx, raw, place, mask, qS, kS, vS):
        ends = [0, self.KP, self.KP + self.NT * HD, self.KP + self.NT * HD + 2 * self.QW]
        self.k_raw, self.v_raw, self.q_raw = (raw[:, a:b] for a, b in zip(ends, ends[1:]))
        rows = S // P
        self.minus_mask = place[:, 0:rows * self.KP].rearrange("p (r n) -> p r n", r=rows)
        self.p_even = place[:, rows * self.KP:(rows + 4) * self.KP].rearrange("p (j n) -> p j n", j=4)
        self.mask, self.qS, self.kS, self.vS = mask, qS, kS, vS
        self.mask_in, self.k_in, self.q_in, self.v_in = (ctx.enter_context(nc.semaphore(name)) for name in
                                                         ("mask_in", "k_in", "q_in", "v_in"))

    def load_kq(self, sp, item):
        sp.dma_start(self.k_raw[:, 0:KV], self.kS[item % G, :, bass.ds(item // G * KV, KV)]).then_inc(self.k_in, 16)
        sp.dma_start(self.q_raw, self.qS[item]).then_inc(self.q_in, 16)

    def load_v(self, sp, item):
        NT, KR = self.NT, self.KR
        sp.dma_start(self.v_raw[:, 0:(NT - 1) * HD].rearrange("p (t d) -> p t d", d=HD),
                     self.vS[bass.ds(item // G * KV, KV - KR), bass.ds(item % G * HD, HD)
                             ].rearrange("(t p) d -> p t d", p=P)).then_inc(self.v_in, 16)

    def load_last_v(self, sp, item):
        NT, KR = self.NT, self.KR
        sp.dma_start(self.v_raw[0:KR, (NT - 1) * HD:NT * HD],
                     self.vS[bass.ds(item // G * KV + (KV - KR), KR), bass.ds(item % G * HD, HD)]
                     ).then_inc(self.v_in, 16)

    def first_loads(self, sp):
        begin_dma(sp, self.k_in, self.q_in, self.v_in)
        self.load_kq(sp, 0)
        for r in range(S // P):
            sp.dma_start(self.minus_mask[:, r, 0:KV], self.mask[r * P:(r + 1) * P, :]).then_inc(self.mask_in, 16)
        self.load_v(sp, 0)


def attention(nc, psum, ident, inputs, oS, ahead):
    with ExitStack() as ctx:
        def sb(name, shape, dt=F32):
            return ctx.enter_context(nc.sbuf_tensor(name, shape, dt))

        def sem(name):
            return ctx.enter_context(nc.semaphore(name))

        ITEMS = B * G
        UNITS = 2 * ITEMS
        QT = 4
        QW = QT * P
        SB, SW, KP, NT, KR = inputs.SB, inputs.SW, inputs.KP, inputs.NT, inputs.KR
        LAG = 3
        TB = 3
        RING = 4
        BODY = 4
        TRIPS = UNITS // BODY
        AT = {0: 1, 2: 2, 5: 3, 10: 0}
        INVERT_AT = {0: 0, 3: 1, 5: 2, 8: 3}
        BY_VECTOR = sorted((at + 1 + LAG) % NT for at in AT)
        BY_SCALAR = [kt for kt in range(NT) if kt not in BY_VECTOR]
        assert NT * BODY % RING == 0 and KP >= KV + KV % 2

        k_raw, v_raw, q_raw, minus_mask = inputs.k_raw, inputs.v_raw, inputs.q_raw, inputs.minus_mask
        q_hi = sb("q_hi", [P, 2, 2 * QW], F32R)
        q_lo = sb("q_lo", [P, 2, 2 * QW], F32R)
        k_hi = sb("k_hi", [P, 2, KP], F32R)
        k_lo = sb("k_lo", [P, 2, KP], F32R)
        v_hi = sb("v_hi", [P, 2, NT * HD], F32R)
        v_lo = sb("v_lo", [P, 2, NT * HD], F32R)
        p_sb = inputs.p_even, sb("p_odd", [P, QT, KP])
        t_min = sb("t_min", [P, 2 * QT])
        p_sum = sb("p_sum", [P, 2 * QT])
        p_inv = sb("p_inv", [P, 2 * QT])
        pT_hi = sb("pT_hi", [P, RING, QW], F32R)
        pT_lo = sb("pT_lo", [P, RING, QW], F32R)
        o_sb = sb("o_sb", [P, 2, QW])

        def t_bank(m):
            return psum[:, SB + m % (NT * BODY) % TB, :]

        mask_in, k_in, q_in, v_in = inputs.mask_in, inputs.k_in, inputs.q_in, inputs.v_in
        pads, mask_done = sem("pads_a"), sem("mask_done")
        kq_hi, kq_lo = sem("kq_hi"), sem("kq_lo")
        v_hi_done, v_lo_done = sem("v_hi_done"), sem("v_lo_done")
        s_done = sem("s_done_a")
        t_done, e_done, inv_done, p_done = sem("t_done"), sem("e_done"), sem("inv_done"), sem("p_done_a")
        pT_done, pT_lo_done = sem("pT_done"), sem("pT_lo_done")
        pT_hi_act, pT_hi_dve = sem("pT_hi_act"), sem("pT_hi_dve")
        pv_done = sem("pv_done")
        o_done = sem("o_done")
        o_out = [sem(f"o_out{s}") for s in range(2)]
        pool_passed, dve_passed = sem("pool_passed_a"), sem("dve_passed_a")

        def s_bank(spare):
            return SB * spare

        o_ps = psum[:, SB + TB, :]

        def banked(ap):
            return ap.rearrange("p (b n) -> p b n", b=SB)

        def rows(kt):
            return P if kt < NT - 1 else KR

        def schedule(eng, position):
            with eng.Fori(0, TRIPS - 1) as i:
                for u in range(BODY):
                    for kt in range(NT):
                        position(i, u, kt)
            for u in range(BODY):
                for kt in range(NT):
                    position(TRIPS - 1, u, kt)

        def last_trip(i):
            return isinstance(i, int) and i == TRIPS - 1

        def exists(i, u):
            return u < BODY or not last_trip(i)

        def scored(u, kt):
            return (u + 1, AT[kt]) if AT[kt] else (u + 2, 0)

        def transposed(u, kt):
            return (u, kt + LAG) if kt + LAG < NT else (u + 1, kt + LAG - NT)

        def tile(i, u, j):
            return QT * (BODY * i + u) + j

        def key_step(i, u, kt):
            return NT * (BODY * i + u) + kt

        def share_step(i, u, kt, share):
            return len(share) * (BODY * i + u) + share.index(kt)

        KQ = [(k_raw, k_hi, k_lo, slice(0, KP // 2)), (k_raw, k_hi, k_lo, slice(KP // 2, KP)),
              (q_raw, q_hi, q_lo, slice(0, 2 * QW))]
        V = [(v_raw, v_hi, v_lo, slice(0, NT * HD // 2)), (v_raw, v_hi, v_lo, slice(NT * HD // 2, NT * HD))]
        SPLIT_AT = {1: 0, 4: 1, 9: 2}

        def splits(i, u, kt, kq, v):
            if kt not in SPLIT_AT:
                return
            if u % 2 and not last_trip(i):
                kq(2 * i + u // 2 + 2, u // 2 % 2, SPLIT_AT[kt])
            if not u % 2 and SPLIT_AT[kt] < len(V) and not (last_trip(i) and u):
                v(2 * i + u // 2 + 1, (u // 2 + 1) % 2, SPLIT_AT[kt])

        block = ctx.enter_context(nc.Block())

        @block.sync
        def _(sp):
            begin_dma(sp, *o_out)

            def load_kq(item):
                sp.wait_ge(kq_lo, done(len(KQ) * item - 1))
                inputs.load_kq(sp, item)

            def load_v(item):
                sp.wait_ge(v_lo_done, done(len(V) * item - 1))
                inputs.load_v(sp, item)
                inputs.load_last_v(sp, item)

            def position(i, u, kt):
                if kt == 1 and not last_trip(i):
                    if u % 2:
                        load_v(2 * i + u // 2 + 2)
                    else:
                        load_kq(2 * i + u // 2 + 2)
                if last_trip(i) and (u, kt) == (1, 1):
                    sp.wait_ge(kq_lo, done(len(KQ) * ITEMS - 1))
                    sp.wait_ge(v_lo_done, done(len(V) * ITEMS - 1))
                    sp.wait_ge(o_out[0], landed((B - 1) * (UNITS // B) // 2))
                    ahead(sp)
                if kt == NT - 1:
                    sp.wait_ge(o_done, done(BODY * i + u))
                    sp.dma_start(oS[BODY * i + u], o_sb[:, u % 2]).then_inc(o_out[u % 2], 16)

            sp.wait_ge(pads, 3)
            inputs.load_last_v(sp, 0)
            load_kq(1)
            load_v(1)
            schedule(sp, position)
            for s in range(2):
                sp.wait_ge(o_out[s], landed(UNITS // 2 - 1))

        @block.gpsimd
        def _(pool):
            begin(pool, kq_lo, v_lo_done, p_done)
            pool.memset(k_raw[:, KV:KP], 0.0).then_inc(pads, 1)
            pool.wait_ge(pads, 1)
            pool.memset(minus_mask[:, :, KV:KP], 3.4028235e38).then_inc(pads, 1)
            pool.wait_ge(pads, 2)
            pool.memset(v_raw[P // 2:P, (NT - 1) * HD:NT * HD], 0.0).then_inc(pads, 1)
            pool.wait_ge(pads, 3)

            def split(hi_done, lo_done, parts):
                def do(item, slot, n):
                    raw, hi, lo, at = parts[n]
                    pool.wait_ge(hi_done, done(len(parts) * item + n))
                    pool.tensor_tensor(lo[:, slot, at], raw[:, at], hi[:, slot, at].bitcast(F32), ALU.subtract
                                       ).then_inc(lo_done, 1)
                return do

            split_kq, split_v = split(kq_hi, kq_lo, KQ), split(v_hi_done, v_lo_done, V)

            def norm(i, u, j):
                at = p_sb[u % 2][:, j, 0:KV]
                wait_apart(pool, inv_done, done(tile(i, u, j)), pool_passed)
                n = QT * (u % 2) + j
                pool.tensor_scalar(at, at, p_inv[:, n:n + 1], 1.0, ALU.mult, ALU.mult).then_inc(p_done, 1)

            def position(i, u, kt):
                if kt in INVERT_AT and exists(i, u + 1):
                    norm(i, u + 1, INVERT_AT[kt])
                splits(i, u, kt, split_kq, split_v)

            split_kq(0, 0, 0)
            for j in range(QT):
                norm(0, 0, j)
            for n in range(len(V)):
                split_v(0, 0, n)
            for n in range(len(KQ)):
                split_kq(1, 1, n)
            schedule(pool, position)

        @block.scalar
        def _(act):
            begin(act, kq_hi, v_hi_done, e_done, pT_hi_act, o_done)
            act.wait_ge(pads, 3)

            def split_kq(item, slot, n):
                raw, hi, _, at = KQ[n]
                act.wait_ge(k_in if n < 2 else q_in, landed(item))
                act.wait_ge(s_done, done(QT * 2 * (item - 1) - 1))
                act.copy(hi[:, slot, at], raw[:, at]).then_inc(kq_hi, 1)

            def split_v(item, slot, n):
                raw, hi, _, at = V[n]
                act.wait_ge(v_in, landed(2 * item + 1))
                act.wait_ge(pv_done, done(NT * 2 * (item - 1) - 1))
                act.copy(hi[:, slot, at], raw[:, at]).then_inc(v_hi_done, 1)

            def exp(i, u, j):
                n = QT * (u % 2) + j
                at = p_sb[u % 2][:, j, 0:KV]
                act.wait_ge(t_done, done(tile(i, u, j)))
                act.activation(at, at, ACT.Exp, bias=t_min[:, n:n + 1], scale=-1.0, accum_out=p_sum[:, n:n + 1]
                               ).then_inc(e_done, 1)

            def split_p(i, u, kt):
                if kt in BY_VECTOR:
                    return
                m, n = NT * u + kt, key_step(i, u, kt)
                act.wait_ge(pT_done, done(n))
                act.wait_ge(pv_done, done(n - RING))
                act.copy(pT_hi[0:rows(kt), m % RING], t_bank(m)[0:rows(kt)]).then_inc(pT_hi_act, 1)

            def position(i, u, kt):
                if exists(i, transposed(u, kt)[0]):
                    split_p(i, *transposed(u, kt))
                if kt == NT - 1:
                    act.wait_ge(pv_done, done(key_step(i, u, kt)))
                    act.wait_ge(o_out[u % 2], landed(BODY // 2 * i + u // 2 - 1))
                    act.copy(o_sb[:, u % 2], o_ps).then_inc(o_done, 1)
                if kt in AT and exists(i, scored(u, kt)[0]):
                    exp(i, *scored(u, kt))
                splits(i, u, kt, split_kq, split_v)

            for n in range(len(KQ)):
                split_kq(0, 0, n)
            for j in range(QT):
                exp(0, 0, j)
            for n in range(len(V)):
                split_v(0, 0, n)
            for n in range(len(KQ)):
                split_kq(1, 1, n)
            exp(0, 1, 0)
            for kt in range(LAG):
                split_p(0, 0, kt)
            schedule(act, position)

        @block.vector
        def _(dve):
            begin(dve, t_done, inv_done, pT_hi_dve, pT_lo_done)
            for n in range(1, len(KQ)):
                raw, hi, lo, at = KQ[n]
                dve.wait_ge(kq_hi, done(n))
                dve.tensor_tensor(lo[:, 0, at], raw[:, at], hi[:, 0, at].bitcast(F32), ALU.subtract).then_inc(kq_lo, 1)
            dve.wait_ge(mask_in, 16 * (S // P))
            dve.tensor_scalar(minus_mask[:, :, 0:KV], minus_mask[:, :, 0:KV], -1.0, None, ALU.mult
                              ).then_inc(mask_done, 1)
            dve.wait_ge(mask_done, 1)
            dve.wait_ge(pads, 2)

            def subtract_mask(i, u, j, spare=0):
                n = QT * (u % 2) + j
                wait_apart(dve, s_done, done(tile(i, u, j)), dve_passed)
                dve.tensor_tensor_reduce(banked(p_sb[u % 2][:, j]),
                                         psum[:, s_bank(spare):s_bank(spare) + SB, 0:SW], banked(minus_mask[:, j % 2]), 1.0,
                                         3.4028235e38, ALU.add, ALU.min, t_min[:, n:n + 1]).then_inc(t_done, 1)

            def invert(i, u, j):
                n = QT * (u % 2) + j
                dve.wait_ge(e_done, done(tile(i, u, j)))
                dve.reciprocal(p_inv[:, n:n + 1], p_sum[:, n:n + 1]).then_inc(inv_done, 1)

            def split_p(i, u, kt):
                m, n = NT * u + kt, key_step(i, u, kt)
                if kt in BY_VECTOR:
                    dve.wait_ge(pT_done, done(n))
                    dve.wait_ge(pv_done, done(n - RING))
                    dve.tensor_copy(pT_hi[0:rows(kt), m % RING], t_bank(m)[0:rows(kt)]).then_inc(pT_hi_dve, 1)
                    dve.wait_ge(pT_hi_dve, done(share_step(i, u, kt, BY_VECTOR)))
                else:
                    dve.wait_ge(pT_hi_act, done(share_step(i, u, kt, BY_SCALAR)))
                dve.tensor_tensor(pT_lo[0:rows(kt), m % RING], t_bank(m)[0:rows(kt)],
                                  pT_hi[0:rows(kt), m % RING].bitcast(F32), ALU.subtract).then_inc(pT_lo_done, 1)

            def position(i, u, kt):
                if kt in INVERT_AT and exists(i, u + 1):
                    invert(i, u + 1, INVERT_AT[kt])
                if kt in AT and exists(i, scored(u, kt)[0]):
                    subtract_mask(i, *scored(u, kt))
                if exists(i, transposed(u, kt)[0]):
                    split_p(i, *transposed(u, kt))

            subtract_mask(0, 0, 0)
            for j in range(1, QT):
                subtract_mask(0, 0, j, j % 2)
                invert(0, 0, j - 1)
            invert(0, 0, QT - 1)
            subtract_mask(0, 1, 0)
            for kt in range(LAG):
                split_p(0, 0, kt)
            schedule(dve, position)

        @block.tensor
        def _(pe):
            begin(pe, s_done, pT_done, pv_done)

            def score(i, u, j, spare=0, former=1):
                slot, q = u // 2 % 2, slice(QW * (u % 2) + P * j, QW * (u % 2) + P * (j + 1))
                if j == 0 and u % 2 == 0:
                    pe.wait_ge(kq_lo, done(len(KQ) * (2 * i + u // 2 + 1) - 1))
                pe.wait_ge(t_done, done(tile(i, u, j) - former))
                for b in range(SB):
                    k = slice(SW * b, SW * (b + 1))
                    last = product(pe, psum[:, s_bank(spare) + b, 0:SW], q_hi[:, slot, q], q_lo[:, slot, q],
                                   k_hi[:, slot, k], k_lo[:, slot, k], True, True)
                last.then_inc(s_done, 1)

            def transpose_p(i, u, kt):
                m, n = NT * u + kt, key_step(i, u, kt)
                if kt == 0:
                    pe.wait_ge(p_done, done(tile(i, u, QT - 1)))
                pe.wait_ge(pT_lo_done, done(n - 1 if m % (NT * BODY) == 0 else n - TB))
                for j in range(QT):
                    last = pe.transpose(t_bank(m)[0:rows(kt), P * j:P * (j + 1)],
                                        p_sb[u % 2][:, j, P * kt:P * kt + rows(kt)], ident)
                last.then_inc(pT_done, 1)

            def weigh_values(i, u, kt):
                m, n, slot = NT * u + kt, key_step(i, u, kt), u // 2 % 2
                r, d = rows(kt), slice(HD * kt, HD * (kt + 1))
                if kt == 0:
                    pe.wait_ge(v_lo_done, done(len(V) * (2 * i + u // 2 + 1) - 1))
                    pe.wait_ge(o_done, done(BODY * i + u - 1))
                pe.wait_ge(pT_lo_done, done(n))
                product(pe, o_ps, v_hi[0:r, slot, d], v_lo[0:r, slot, d], pT_hi[0:r, m % RING], pT_lo[0:r, m % RING],
                        kt == 0, kt == NT - 1).then_inc(pv_done, 1)

            def position(i, u, kt):
                if kt in AT and exists(i, scored(u, kt)[0]):
                    score(i, *scored(u, kt))
                weigh_values(i, u, kt)
                if exists(i, transposed(u, kt)[0]):
                    transpose_p(i, *transposed(u, kt))

            for j in range(QT):
                score(0, 0, j, j % 2, 2)
            score(0, 1, 0)
            for kt in range(LAG):
                transpose_p(0, 0, kt)
            schedule(pe, position)


class OutputInputs:

    def __init__(self, nc, ctx, raw, oS, WoT):
        n = 2 * D
        self.w_raw = raw[:, 0:2 * n].rearrange("p (r h n) -> p r h n", r=2, h=2)
        self.o_raw = [raw[:, 2 * n:2 * n + 2 * B * S].rearrange("p (b n) -> p b n", b=B)]
        self.o_view = oS.rearrange("(b h) d n -> h d b n", b=B)
        self.WoT = WoT
        self.o_in = [ctx.enter_context(nc.semaphore(f"o_in{s}")) for s in range(2)]
        self.w_in = [ctx.enter_context(nc.semaphore(f"wo_in{s}")) for s in range(2)]

    def load_w(self, sp, pair, r):
        sp.dma_start(self.w_raw[:, r], cols(self.WoT)[:, bass.ds(2 * pair, 2), :]).then_inc(self.w_in[r], 16)

    def load_o(self, sp, pair, r):
        sp.dma_start(self.o_raw[r], self.o_view[pair]).then_inc(self.o_in[r], 16)

    def first_loads(self, sp):
        begin_dma(sp, *self.o_in, *self.w_in)
        self.load_w(sp, 0, 0)
        self.load_o(sp, 0, 0)


def output_and_experts(nc, psum, ident, inputs, x1S, AT, routeT, BwT, out):
    with ExitStack() as ctx:
        def sb(name, shape, dt=F32):
            return ctx.enter_context(nc.sbuf_tensor(name, shape, dt))

        def sem(name):
            return ctx.enter_context(nc.semaphore(name))

        PAIRS = H // 2
        W = 2 * S
        PIECES = B + 1
        w_raw = inputs.w_raw
        o_raw = inputs.o_raw + [sb("o_raw", [P, B, W])[:]]
        inputs.o_raw = o_raw
        o_hi = sb("o_hi", [P, 2, B, W], F32R)
        o_lo = sb("o_lo", [P, 2, B, W], F32R)
        w_hi = sb("wo_hi", [P, 2, 2, D], F32R)
        w_lo = sb("wo_lo", [P, 2, 2, D], F32R)
        x1_sb = sb("x1_in", [P, TT, D])
        expert_in = sb("expert_in", [P, CT, E * R + E])
        expert_out = sb("expert_out", [P, D])
        y_sb = sb("y_sb", [P, TT, D])
        stats = sb("stats", [P, TT, 6])
        mv = sb("mv", [P, TT, 2])
        rstd = sb("rstd_f", [P, TT])
        minus_half = sb("minus_half_f", [P, 1])
        x2_sb = sb("x2_sb", [P, TT, D])
        x2T_sb = sb("x2T_sb", [P, TT, D])
        rank = sb("rank", [P, E])
        best = sb("best", [P, TT])
        ranked = sb("ranked", [P, TT, E])
        first = sb("first", [P, TT])
        route = sb("route", [P, TT, E])
        wh_sb = sb("wh_sb", [P, TT, E * R])
        whT_sb = sb("whT_sb", [P, TT, P])
        out_sb = sb("out_sb", [P, TT, D])

        o_in, w_in = inputs.o_in, inputs.w_in
        x1_in, expert_loaded, consts = sem("x1_in_done"), sem("expert_loaded"), sem("consts")
        hi_done, lo_done = sem("hi_done_f"), sem("lo_done_f")
        pair_done = sem("pair_done")
        sum_done = sem("sum_done")
        chain, mv_done, rstd_done, x2_done = sem("chain_f"), sem("mv_done_f"), sem("rstd_done_f"), sem("x2_done")
        x2T_done, x2T_sb_done, h_done, wh_done = sem("x2T_done"), sem("x2T_sb_done"), sem("h_done_f"), sem("wh_done")
        whT_done, whT_sb_done, f_done = sem("whT_done"), sem("whT_sb_done"), sem("f_done")
        out_done, out_out = sem("out_done"), sem("out_out")

        def pairs(eng, step):
            step(0, 0, True, False)
            with eng.Fori(0, PAIRS // 2 - 1) as i:
                step(i, 1, False, False)
                step(i + 1, 0, False, False)
            step(PAIRS // 2 - 1, 1, False, True)

        def bank(t):
            return psum[:, t, :]

        block = ctx.enter_context(nc.Block())

        @block.sync
        def _(sp):
            def load(i, r, *_):
                first = isinstance(i, int) and 2 * i + r == 0
                if not first:
                    sp.wait_ge(lo_done, done(PIECES * (2 * i + r - 1) - 1))
                    inputs.load_w(sp, 2 * i + r, r)
                    inputs.load_o(sp, 2 * i + r, r)

            pairs(sp, load)
            sp.dma_start(x1_sb[:], cols(x1S)).then_inc(x1_in, 16)
            sp.dma_start(expert_in[:, :, 0:E * R], cols(AT)).then_inc(expert_loaded, 16)
            sp.dma_start(expert_in[:, :, E * R:E * R + E], cols(routeT)).then_inc(expert_loaded, 16)
            sp.dma_start(expert_out[:], BwT).then_inc(expert_loaded, 16)

            for s in range(TT):
                sp.wait_ge(out_done, done(s))
                sp.dma_start(out[s * P:(s + 1) * P, :], out_sb[:, s]).then_inc(out_out, 16)

            sp.wait_ge(out_out, 16 * TT)

        @block.gpsimd
        def _(pool):
            begin(pool, rstd_done)
            pool.memset(minus_half[:], -0.5).then_inc(consts, 1)
            for e in range(E):
                pool.memset(rank[:, e:e + 1], float(E - e)).then_inc(consts, 1)
            pool.wait_ge(consts, 1)

            for norm in range(2):
                for s in range(TT):
                    n = TT * norm + s
                    pool.wait_ge(mv_done, done(n))
                    pool.tensor_tensor(rstd[:, s:s + 1], mv[:, s, 1:2], minus_half[:], ALU.pow
                                       ).then_inc(rstd_done, 1)

        @block.scalar
        def _(act):
            begin(act, hi_done, x2T_sb_done, whT_sb_done)

            def split(i, r, *_):
                act.wait_ge(w_in[r], landed(i))
                act.wait_ge(pair_done, done(2 * i + r - 2))
                act.copy(w_hi[:, r], w_raw[:, r]).then_inc(hi_done, 1)
                act.wait_ge(o_in[r], landed(i))
                for b in range(B):
                    act.copy(o_hi[:, r, b], o_raw[r][:, b]).then_inc(hi_done, 1)

            pairs(act, split)

            for s in range(TT):
                act.wait_ge(x2T_done, done(s))
                act.copy(x2T_sb[:, s], bank(s)).then_inc(x2T_sb_done, 1)
            for s in range(TT):
                act.wait_ge(whT_done, done(s))
                act.copy(whT_sb[:, s], bank(s)[:, 0:P]).then_inc(whT_sb_done, 1)

        @block.vector
        def _(dve):
            begin(dve, lo_done, mv_done, x2_done, wh_done, out_done)

            def split(i, r, *_):
                n = PIECES * (2 * i + r)
                dve.wait_ge(hi_done, done(n))
                dve.tensor_tensor(w_lo[:, r], w_raw[:, r], w_hi[:, r].bitcast(F32), ALU.subtract
                                  ).then_inc(lo_done, 1)
                for b in range(B):
                    dve.wait_ge(hi_done, done(n + 1 + b))
                    dve.tensor_tensor(o_lo[:, r, b], o_raw[r][:, b], o_hi[:, r, b].bitcast(F32), ALU.subtract
                                      ).then_inc(lo_done, 1)

            pairs(dve, split)
            dve.wait_ge(x1_in, 16)
            dve.wait_ge(consts, 1 + E)
            own = Chain(dve, chain)

            def moments(s, increase, x):
                own.done(dve.tensor_tensor(y_sb[:, s], increase, x, ALU.add))
                own.wait()
                own.done(dve.bn_stats(stats[:, s], y_sb[:, s]))
                own.wait()
                own.done(dve.bn_aggr(mv[:, s], stats[:, s]))
                own.wait()
                dve.tensor_scalar(mv[:, s, 1:2], mv[:, s, 1:2], EPS, None, ALU.add).then_inc(mv_done, 1)

            def norm(n, s, to, ready):
                dve.wait_ge(rstd_done, done(n))
                dve.tensor_scalar(to, y_sb[:, s], mv[:, s, 0:1], rstd[:, s:s + 1], ALU.subtract, ALU.mult
                                  ).then_inc(ready, 1)

            def weigh(s):
                logits = bank(s)[:, E * R:E * R + E]
                dve.wait_ge(h_done, done(s))
                own.done(dve.tensor_reduce(best[:, s:s + 1], logits, mybir.AxisListType.X, ALU.max))
                own.wait()
                own.done(dve.scalar_tensor_tensor(ranked[:, s], logits, best[:, s:s + 1], rank[:], ALU.is_equal,
                                                  ALU.mult))
                own.wait()
                own.done(dve.tensor_reduce(first[:, s:s + 1], ranked[:, s], mybir.AxisListType.X, ALU.max))
                own.wait()
                own.done(dve.tensor_scalar(route[:, s], ranked[:, s], first[:, s:s + 1], best[:, s:s + 1],
                                           ALU.is_equal, ALU.mult))
                own.wait()
                dve.tensor_tensor(wh_sb[:, s].rearrange("p (e r) -> p e r", e=E),
                                  bank(s)[:, 0:E * R].rearrange("p (e r) -> p e r", e=E),
                                  route[:, s].unsqueeze(2).to_broadcast((P, E, R)), ALU.mult).then_inc(wh_done, 1)

            for s in range(TT):
                dve.wait_ge(sum_done, done(s))
                moments(s, bank(s), x1_sb[:, s])
                if s:
                    norm(s - 1, s - 1, x2_sb[:, s - 1], x2_done)
            norm(TT - 1, TT - 1, x2_sb[:, TT - 1], x2_done)
            for s in range(TT):
                weigh(s)
            for s in range(TT):
                dve.wait_ge(f_done, done(s))
                moments(s, bank(s), x2_sb[:, s])
                if s:
                    norm(TT + s - 1, s - 1, out_sb[:, s - 1], out_done)
            norm(2 * TT - 1, TT - 1, out_sb[:, TT - 1], out_done)

        @block.tensor
        def _(pe):
            begin(pe, pair_done, sum_done, x2T_done, h_done, whT_done, f_done)

            def multiply(i, r, start, stop):
                for b in range(B):
                    pe.wait_ge(lo_done, done(PIECES * (2 * i + r) + 1 + b))
                    for j in range(S // P):
                        for h in range(2):
                            q = slice(h * S + j * P, h * S + (j + 1) * P)
                            last = product(pe, psum[:, b * (S // P) + j, :], o_hi[:, r, b, q], o_lo[:, r, b, q],
                                           w_hi[:, r, h], w_lo[:, r, h], start and h == 0, stop and h == 1)
                        if stop:
                            last.then_inc(sum_done, 1)
                if not stop:
                    last.then_inc(pair_done, 1)

            pairs(pe, multiply)
            pe.wait_ge(expert_loaded, 48)

            for s in range(TT):
                pe.wait_ge(x2_done, done(s))
                for c in range(CT):
                    last = pe.transpose(bank(s)[:, c * P:(c + 1) * P], x2_sb[:, s, c * P:(c + 1) * P], ident)
                last.then_inc(x2T_done, 1)
            for s in range(TT):
                pe.wait_ge(x2T_sb_done, done(s))
                for c in range(CT):
                    last = pe.matmul(bank(s)[:, 0:E * R + E], x2T_sb[:, s, c * P:(c + 1) * P],
                                     expert_in[:, c], start=c == 0, stop=c == CT - 1)
                last.then_inc(h_done, 1)
            for s in range(TT):
                pe.wait_ge(wh_done, done(s))
                pe.transpose(bank(s)[:, 0:P], wh_sb[:, s], ident).then_inc(whT_done, 1)
            for s in range(TT):
                pe.wait_ge(whT_sb_done, done(s))
                pe.matmul(bank(s), whT_sb[:, s], expert_out[:], start=True, stop=True).then_inc(f_done, 1)



def decoder_layer(nc, x, xT, ctxT, mask, WgT, WuT, WdT, WqT, WkT, WvT, WoT, qn, kn, routeT, AT, BwT, out):
    pS = nc.dram_tensor("gated_products", (TT, P, I), F32).ap()
    kS = nc.dram_tensor("keys", (G, HD, NK), F32).ap()
    vS = nc.dram_tensor("values", (NK, G * HD), F32).ap()
    x1S = nc.dram_tensor("x1", (T, D), F32).ap()
    qS = nc.dram_tensor("queries", (B, G, HD, H // G, S), F32).ap()
    oS = nc.dram_tensor("attended", (B * H // 2, HD, 2 * S), F32).ap()
    with ExitStack() as whole:
        psum = whole.enter_context(nc.psum_tensor("banks", [P, 8, 512], F32))
        ident = whole.enter_context(nc.sbuf_tensor("ident", [P, P], F32))[:]
        raw = whole.enter_context(nc.sbuf_tensor("raw", [P, IC * D], F32))[:]
        make_identity(nc, ident)
        output_inputs = OutputInputs(nc, whole, raw, oS, WoT)
        with ExitStack() as front:
            abs_s = front.enter_context(nc.sbuf_tensor("abs_s", [P, TT, I], F32))
            attention_inputs = AttentionInputs(nc, front, raw, abs_s[:].rearrange("p t n -> p (t n)"), mask,
                                               qS.rearrange("b g d h q -> (b g) d (h q)"), kS, vS)
            with ExitStack() as ctx:
                thr = ctx.enter_context(nc.sbuf_tensor("thr", [P, TT], U32))
                n_less = ctx.enter_context(nc.sbuf_tensor("n_less", [P, TT], F32))
                kv_weights = KeyValueWeights(nc, ctx, raw, WkT, WvT)
                gate_and_up(nc, psum, raw, abs_s, xT, WgT, WuT, pS, kv_weights.first_loads)
                down_inputs = DownInputs(nc, ctx, raw, x, WdT, pS)
                keys_and_values(nc, psum, ident, abs_s, thr, n_less, kv_weights, ctxT, kS, vS,
                                down_inputs.first_loads)
                x1T_hi = ctx.enter_context(nc.sbuf_tensor("x1T_hi", [P, CT, T], F32R))
                x1T_lo = ctx.enter_context(nc.sbuf_tensor("x1T_lo", [P, CT, T], F32R))
                query_weights = QueryWeights(nc, ctx, raw, WqT)
                down_and_norm(nc, psum, ident, abs_s, thr, n_less, x1T_hi, x1T_lo, down_inputs, x1S,
                              query_weights.first_loads)
                queries(nc, psum, ident, x1T_hi, x1T_lo, query_weights, qn, kn, qS, attention_inputs.first_loads)
            attention(nc, psum, ident, attention_inputs, oS, output_inputs.first_loads)
        output_and_experts(nc, psum, ident, output_inputs, x1S, AT, routeT, BwT, out)


def kernel(x, ctx_4096, mask_1x1xSxS2_ff0, L0_attn_w_gate, L0_attn_w_up, L0_attn_w_down, L0_xattn_Wq, L0_xattn_Wk,
           L0_xattn_Wv, L0_xattn_Wo, L0_xattn_q_norm_w, L0_xattn_k_norm_w, L0_ffn_route_w, L0_ffn_A, L0_ffn_Bw):
    import numpy as np
    import concourse.bacc as bacc
    from concourse.bass_utils import run_bass_kernel_spmd

    def transposed(a, rows):
        return np.ascontiguousarray(np.asarray(a).reshape(rows, -1).T)

    x = np.asarray(x).reshape(T, D)
    arrays = {
        "x": np.ascontiguousarray(x),
        "xT": transposed(x, T),
        "ctxT": transposed(ctx_4096, NK),
        "mask": np.ascontiguousarray(np.asarray(mask_1x1xSxS2_ff0).reshape(S, KV)),
        "WgT": transposed(L0_attn_w_gate, I),
        "WuT": transposed(L0_attn_w_up, I),
        "WdT": transposed(L0_attn_w_down, D),
        "WqT": transposed(L0_xattn_Wq, H * HD),
        "WkT": transposed(L0_xattn_Wk, G * HD),
        "WvT": transposed(L0_xattn_Wv, G * HD),
        "WoT": transposed(L0_xattn_Wo, D),
        "qn": np.ascontiguousarray(np.asarray(L0_xattn_q_norm_w).reshape(HD, 1)),
        "kn": np.ascontiguousarray(np.asarray(L0_xattn_k_norm_w).reshape(HD, 1)),
        "routeT": transposed(L0_ffn_route_w, E),
        "AT": transposed(L0_ffn_A, E * R),
        "BwT": np.ascontiguousarray(np.asarray(L0_ffn_Bw).transpose(0, 2, 1).reshape(E * R, D)),
    }
    nc = bacc.Bacc("TRN2", target_bir_lowering=False, num_devices=1)
    args = {name: nc.dram_tensor(name + "_in", a.shape, mybir.dt.from_np(a.dtype), kind="ExternalInput").ap()
            for name, a in arrays.items()}
    out = nc.dram_tensor("out", (T, D), F32, kind="ExternalOutput").ap()
    decoder_layer(nc, out=out, **args)
    r = run_bass_kernel_spmd(nc, [{name + "_in": a for name, a in arrays.items()}], core_ids=[0])
    return r.results[0]["out"].reshape(B, S, D)
```
